# Optimizing a Trainium2 kernel written in Bass

```python
import numpy as np
import jax
import jax.numpy as jnp

def _softmax(x, axis=-1):
    return jax.nn.softmax(x, axis=axis)

def _gelu(x):
    return jax.nn.gelu(x, approximate=True)

def _silu(x):
    return jax.nn.silu(x)

def _sigmoid(x):
    return jax.nn.sigmoid(x)

def _layernorm(x, axis=-1, eps=1e-05):
    m = jnp.mean(x, axis=axis, keepdims=True)
    v = jnp.var(x, axis=axis, keepdims=True)
    return (x - m) / jnp.sqrt(v + eps)

def _scatter_add(tgt, idx, src, axis=0):
    return tgt.at[idx].add(src)

def _segment_sum(src, seg, n):
    return jax.ops.segment_sum(src, seg, n)
kernel_name = 'mk_flamingo_gated_d1_seqx_r4_e969a6'

def setup_inputs(seed: int=0):
    np.random.seed(seed)
    _w = jnp.asarray

    def _rec_inputs():
        import jax
        import jax.numpy as jnp
        _rk = jax.random.key(seed)
        x = -0.0002928 + 1 * jax.random.normal(jax.random.fold_in(_rk, 1), (4, 512, 256), jnp.float32)
        _lenS = 512 - jax.random.randint(jax.random.fold_in(_rk, 7), (4,), 0, max(1, 512 // 4) + 1, jnp.int32)
        _lenS2 = 512 - jax.random.randint(jax.random.fold_in(_rk, 8), (4,), 0, max(1, 512 // 4) + 1, jnp.int32)
        _ctx_1024P = jax.random.normal(jax.random.fold_in(_rk, 11), (4, 16, 256), jnp.float32)
        _ctx_1024c = jax.random.dirichlet(jax.random.fold_in(_rk, 511), 0.3 * jnp.ones((16,), jnp.float32), (4, 512))
        _ctx_1024t = jnp.einsum('bsk,bkd->bsd', _ctx_1024c, _ctx_1024P)
        _ctx_1024t = _ctx_1024t * jax.lax.rsqrt(jnp.mean(jnp.square(_ctx_1024t)) + 1e-12) * 0.953939
        ctx_1024 = -1.39393e-06 + 0.999914 * (_ctx_1024t + 0.3 * jax.random.normal(jax.random.fold_in(_rk, 611), (4, 512, 256), jnp.float32))
        _g = jax.random.normal(jax.random.fold_in(_rk, 9001), (2, 1), jnp.float32)
        _g = jnp.sign(_g) * jnp.maximum(jnp.abs(_g), 1.0) + (_g == 0) * 1.0
        g_xattn = _g[0]
        g_ffn = _g[1]
        return (x, ctx_1024, g_xattn, g_ffn)
    x, ctx_1024, g_xattn, g_ffn = _rec_inputs()

    def _L0_xattn_setup():
        import jax, jax.numpy as jnp
        import numpy as np
        B, S, D, NH = (2, 512, 256, 8)
        DH = D // NH
        EPS = 1e-06
        LN_EPS = 1e-05

        def _mlstm_cell(q, k, v, igate_w, igate_b, fgate_w, fgate_b, ln_scale):
            Slen = q.shape[0]
            ifg = jnp.concatenate([q, k, v], axis=-1)
            ig = (ifg @ igate_w.T + igate_b).T
            fg = (ifg @ fgate_w.T + fgate_b).T
            qh = q.reshape(Slen, NH, DH).transpose(1, 0, 2)
            kh = k.reshape(Slen, NH, DH).transpose(1, 0, 2)
            vh = v.reshape(Slen, NH, DH).transpose(1, 0, 2)
            log_f = jax.nn.log_sigmoid(fg)
            cs = jnp.cumsum(log_f, axis=1)
            fg_mat = cs[:, :, None] - cs[:, None, :]
            mask = jnp.tril(jnp.ones((Slen, Slen), dtype=bool))
            log_fg_mat = jnp.where(mask, fg_mat, -jnp.inf)
            log_D = log_fg_mat + ig[:, None, :]
            max_log_D = jnp.max(log_D, axis=-1, keepdims=True)
            D_mat = jnp.exp(log_D - max_log_D)
            qk = jnp.einsum('hsd,htd->hst', qh, kh) / np.sqrt(DH)
            C = qk * D_mat
            normalizer = jnp.maximum(jnp.abs(C.sum(axis=-1, keepdims=True)), jnp.exp(-max_log_D))
            h = jnp.einsum('hst,htd->hsd', C / (normalizer + EPS), vh)
            h = h.transpose(1, 0, 2).reshape(Slen, D)
            mu = h.mean(axis=-1, keepdims=True)
            var = h.var(axis=-1, keepdims=True)
            return (h - mu) / jnp.sqrt(var + LN_EPS) * ln_scale
        key = jax.random.key(seed)
        ks = jax.random.split(key, 8)
        rnd = lambda k, sh, s=1.0: jax.random.normal(k, sh, dtype=jnp.float32) * s
        return {'q': rnd(ks[0], (B, S, D)), 'k': rnd(ks[1], (B, S, D)), 'v': rnd(ks[2], (B, S, D)), 'igate_w': rnd(ks[3], (NH, 3 * D), 0.02), 'igate_b': jnp.linspace(3.0, 6.0, NH, dtype=jnp.float32), 'fgate_w': rnd(ks[4], (NH, 3 * D), 0.02), 'fgate_b': rnd(ks[5], (NH,), 0.3162278), 'ln_scale': jnp.ones((D,), dtype=jnp.float32)}
    _L0_xattn_all = _L0_xattn_setup()
    _L0_xattn_in = {k: v for k, v in _L0_xattn_all.items() if k in ('igate_w', 'igate_b', 'fgate_w', 'fgate_b', 'ln_scale')}
    del _L0_xattn_all

    def _L0_ffn_setup():
        import jax, jax.numpy as jnp
        import numpy as np
        E = 8
        K = 2
        D = 256
        H = 256
        B, T = (2, 256)
        key = jax.random.key(seed)
        ks = jax.random.split(key, 6)
        s = 0.02
        return {'x': jax.random.normal(ks[0], (B, T, D), dtype=jnp.float32), 'gate_w': jax.random.normal(ks[1], (E, D), dtype=jnp.float32) * s, 'lb_bias': jnp.zeros((E,), dtype=jnp.float32), 'w1': jax.random.normal(ks[2], (E, H, D), dtype=jnp.float32) * s, 'w2': jax.random.normal(ks[3], (E, D, H), dtype=jnp.float32) * s, 'cfc': jax.random.normal(ks[4], (H, D), dtype=jnp.float32) * s, 'cproj': jax.random.normal(ks[5], (D, H), dtype=jnp.float32) * s}
    _L0_ffn_all = _L0_ffn_setup()
    _L0_ffn_in = {k: v for k, v in _L0_ffn_all.items() if k in ('gate_w', 'lb_bias', 'w1', 'w2', 'cfc', 'cproj')}
    del _L0_ffn_all
    return {'x': x, 'ctx_1024': ctx_1024, 'g_xattn': g_xattn, 'g_ffn': g_ffn, 'L0_xattn_igate_w': _L0_xattn_in['igate_w'], 'L0_xattn_igate_b': _L0_xattn_in['igate_b'], 'L0_xattn_fgate_w': _L0_xattn_in['fgate_w'], 'L0_xattn_fgate_b': _L0_xattn_in['fgate_b'], 'L0_xattn_ln_scale': _L0_xattn_in['ln_scale'], 'L0_ffn_gate_w': _L0_ffn_in['gate_w'], 'L0_ffn_lb_bias': _L0_ffn_in['lb_bias'], 'L0_ffn_w1': _L0_ffn_in['w1'], 'L0_ffn_w2': _L0_ffn_in['w2'], 'L0_ffn_cfc': _L0_ffn_in['cfc'], 'L0_ffn_cproj': _L0_ffn_in['cproj']}

def reference(x, ctx_1024, g_xattn, g_ffn, L0_xattn_igate_w, L0_xattn_igate_b, L0_xattn_fgate_w, L0_xattn_fgate_b, L0_xattn_ln_scale, L0_ffn_gate_w, L0_ffn_lb_bias, L0_ffn_w1, L0_ffn_w2, L0_ffn_cfc, L0_ffn_cproj):
    import jax
    import jax.numpy as jnp

    def _L0_xattn_ref(q, k, v, igate_w, igate_b, fgate_w, fgate_b, ln_scale):
        import jax, jax.numpy as jnp
        import numpy as np
        B, S, D, NH = (2, 512, 256, 8)
        DH = D // NH
        EPS = 1e-06
        LN_EPS = 1e-05

        def _mlstm_cell(q, k, v, igate_w, igate_b, fgate_w, fgate_b, ln_scale):
            Slen = q.shape[0]
            ifg = jnp.concatenate([q, k, v], axis=-1)
            ig = (ifg @ igate_w.T + igate_b).T
            fg = (ifg @ fgate_w.T + fgate_b).T
            qh = q.reshape(Slen, NH, DH).transpose(1, 0, 2)
            kh = k.reshape(Slen, NH, DH).transpose(1, 0, 2)
            vh = v.reshape(Slen, NH, DH).transpose(1, 0, 2)
            log_f = jax.nn.log_sigmoid(fg)
            cs = jnp.cumsum(log_f, axis=1)
            fg_mat = cs[:, :, None] - cs[:, None, :]
            mask = jnp.tril(jnp.ones((Slen, Slen), dtype=bool))
            log_fg_mat = jnp.where(mask, fg_mat, -jnp.inf)
            log_D = log_fg_mat + ig[:, None, :]
            max_log_D = jnp.max(log_D, axis=-1, keepdims=True)
            D_mat = jnp.exp(log_D - max_log_D)
            qk = jnp.einsum('hsd,htd->hst', qh, kh) / np.sqrt(DH)
            C = qk * D_mat
            normalizer = jnp.maximum(jnp.abs(C.sum(axis=-1, keepdims=True)), jnp.exp(-max_log_D))
            h = jnp.einsum('hst,htd->hsd', C / (normalizer + EPS), vh)
            h = h.transpose(1, 0, 2).reshape(Slen, D)
            mu = h.mean(axis=-1, keepdims=True)
            var = h.var(axis=-1, keepdims=True)
            return (h - mu) / jnp.sqrt(var + LN_EPS) * ln_scale
        return jax.vmap(lambda qq, kk, vv: _mlstm_cell(qq, kk, vv, igate_w, igate_b, fgate_w, fgate_b, ln_scale))(q, k, v)

    def _L0_ffn_ref(x, gate_w, lb_bias, w1, w2, cfc, cproj):
        import jax, jax.numpy as jnp
        import numpy as np
        E = 8
        K = 2
        D = 256
        H = 256
        B, T = (2, 256)
        Bx, Tx, Dx = x.shape
        logits = jnp.einsum('btd,ed->bte', x, gate_w)
        _, idx = jax.lax.top_k(logits + lb_bias, K)
        sel_logits = jnp.take_along_axis(logits, idx, axis=-1)
        w = jax.nn.sigmoid(sel_logits)
        w = w / (jnp.sum(w, axis=-1, keepdims=True) + 1e-06)
        xf = x.reshape(-1, Dx)
        idxf = idx.reshape(-1, K)
        wf = w.reshape(-1, K)
        onehot = jax.nn.one_hot(idxf, E, dtype=wf.dtype)
        we = jnp.einsum('nke,nk->ne', onehot, wf)
        hidden = jnp.square(jax.nn.relu(jnp.einsum('nd,ehd->neh', xf, w1)))
        expert_out = jnp.einsum('neh,edh->ned', hidden, w2)
        moe_out = jnp.einsum('ned,ne->nd', expert_out, we).reshape(Bx, Tx, Dx)
        sh = jnp.square(jax.nn.relu(jnp.einsum('btd,hd->bth', x, cfc)))
        shared = jnp.einsum('bth,dh->btd', sh, cproj)
        return moe_out + shared
    x = x + jnp.tanh(g_xattn[0]) * _L0_xattn_ref(_layernorm(x, axis=-1), ctx_1024, ctx_1024, L0_xattn_igate_w, L0_xattn_igate_b, L0_xattn_fgate_w, L0_xattn_fgate_b, L0_xattn_ln_scale)
    x = x + jnp.tanh(g_ffn[0]) * _L0_ffn_ref(_layernorm(x, axis=-1), L0_ffn_gate_w, L0_ffn_lb_bias, L0_ffn_w1, L0_ffn_w2, L0_ffn_cfc, L0_ffn_cproj)
    return x

_drawn_inputs = setup_inputs


def setup_inputs(seed=0):
    import zlib

    import numpy as np

    out = dict(_drawn_inputs(seed))
    spreads = {'L0_xattn_ln_scale': (1.0, 0.2), 'L0_ffn_lb_bias': (0.0, 0.748)}
    factors = {'L0_ffn_gate_w': 3.46, 'L0_ffn_w1': 3.255, 'L0_ffn_w2': 2.963, 'L0_ffn_cfc': 2.683}
    for name, (base, spread) in spreads.items():
        noise = np.random.default_rng([zlib.crc32(name.encode()), seed]).standard_normal(out[name].shape)
        drawn = base * np.exp(spread * noise) if base else spread * noise
        out[name] = jnp.asarray(drawn.astype(out[name].dtype))
    for name, factor in factors.items():
        out[name] = (out[name] * factor).astype(out[name].dtype)
    return out
```

```python
from contextlib import ExitStack

import numpy as np
import concourse.bass as bass
from concourse import mybir

F32 = mybir.dt.float32
BF16 = mybir.dt.bfloat16
ALU = mybir.AluOpType
ACT = mybir.ActivationFunctionType
AX = mybir.AxisListType

P = 128
B, S, D = 4, 512, 256
NH, DH = 8, 32
C = S // P
KC = D // P
NBH = B * NH
HG = NH // 4
DV = DH + 1
GV = 4 * DV
E = 8
NE = E + 1
MIXED = 3
LN_EPS, EPS, W_EPS = 1e-5, 1e-6, 1e-6
SCALE = float(DH) ** -0.5
NEG = -1e30
LOWEST = -3.0e38


def gated_block(nc, x, ctx, ctxT, experts, gate_w, gate_b, row, route_w, out):
    es = ExitStack()
    with es:
        def sb(name, shape, dt=F32):
            return es.enter_context(nc.sbuf_tensor(name, shape, dt))

        def sem(name):
            return es.enter_context(nc.semaphore(name))

        x_all = sb("x_all", [P, B, C, D])
        qT_all = sb("qT_all", [P, B, KC, S])
        kT_all = sb("kT_all", [P, B, KC, S])
        ctx_all = sb("ctx_all", [P, B, C, D])
        vaug = sb("vaug", [P, B, C, NH, DV])
        w_hi = sb("w_hi", [P, NE, 2, KC, D], BF16)
        w_lo = sb("w_lo", [P, NE, 2, KC, D], BF16)
        w_stage = sb("w_stage", [P, 3, 2, KC, D])
        xn = ctx_all
        xT = qT_all
        xT_hi = kT_all[:, 0:2, :, :].rearrange("p a k s -> p (a k s)").bitcast(BF16)\
            .rearrange("p (b k s) -> p b k s", b=B, k=KC)
        xT_lo = kT_all[:, 2:4, :, :].rearrange("p a k s -> p (a k s)").bitcast(BF16)\
            .rearrange("p (b k s) -> p b k s", b=B, k=KC)
        ident = sb("ident", [P, P])
        ident_b = sb("ident_b", [P, P], BF16)
        mask = sb("mask", [P, C, P], BF16)
        zeros_c = sb("zeros_c", [P, C * P], BF16)
        pick_small = sb("pick_small", [96, NBH], BF16)
        pick3 = sb("pick3", [96, NBH, P], BF16)
        spread = sb("spread", [NBH, 2 * B, P])
        block_mask = sb("block_mask", [P, GV])
        neg_half = sb("neg_half", [P, C])
        eps_c = sb("eps_c", [P, C])
        ones_row = sb("ones_row", [NBH, S])
        before = sb("before", [P, E, E])
        consts = sb("consts", [P, D + E + 2])
        tanhs = sb("tanhs", [P, 2])
        ln_gain = sb("ln_gain", [P, D])
        gate_raw = sb("gate_raw", [P, 3 * KC, 2, NH])
        gate_sum = sb("gate_sum", [P, 2 * KC, 2, NH])
        gate_pad = sb("gate_pad", [P, B, 2 * KC, 2 * NBH])
        gate_bias = sb("gate_bias", [NBH, 2])
        route = sb("route", [P, KC, E])
        scratch = w_lo[0:NBH].rearrange("p e a k d -> p (e a k d)").bitcast(F32)
        f_pre, f_abs, log_f, cs = (scratch[:, i * S:(i + 1) * S] for i in range(4))
        am = scratch[:, 4 * S:6 * S].rearrange("p (t s) -> p t s", t=2)
        am_rest = scratch[:, 6 * S:8 * S].rearrange("p (t s) -> p t s", t=2)
        am_mid = scratch[:, 8 * S:9 * S].bitcast(BF16).rearrange("p (t s) -> p t s", t=2)
        am3 = sb("am3", [96, 2, S], BF16)
        rows = sb("rows", [96, S])
        decay_row = sb("decay_row", [NBH, 2])
        decay_exp = sb("decay_exp", [NBH, 2])
        decay = sb("decay", [P, B * HG, 2])
        ex = sb("ex", [P, C, 96])
        st1 = sb("st1", [P, 2, C, 6])
        mv1 = sb("mv1", [P, 2, C, 2])
        rs1 = sb("rs1", [P, 2, C])
        q_tok = sb("q_tok", [P, 2, C, D])
        st2 = sb("st2", [P, C, 6])
        mv2 = sb("mv2", [P, C, 2])
        rs2 = sb("rs2", [P, C])
        kT = sb("kT", [P, KC, S])
        qT = sb("qT", [P, KC, S])
        k_wt = sb("k_wt", [P, C - 1, D])
        d_sb = sb("d_sb", [P, 2, S])
        p_sb = sb("p_sb", [P, 2, S])
        state = sb("state", [P, HG, C - 1, GV])
        carried = sb("carried", [P, C - 1, GV])
        h_sum = sb("h_sum", [P, C, NH, DV])
        norm = sb("norm", [P, 3, C, NH])
        h_n = sb("h_n", [P, C, D])
        relu_z = q_tok[:, :, :, :].rearrange("p a c d -> p a (c d)").rearrange("p a (h s) -> p a h s", h=KC)
        values = vaug[:].rearrange("p b c h d -> p (b c h d)")
        sq = values[:, 0:KC * S].rearrange("p (h s) -> p h s", h=KC)
        sq_hi, sq_lo = (values[:, i * KC * S:(i + 1) * KC * S].bitcast(BF16)
                        .rearrange("p (t h s) -> p t h s", t=2, h=KC) for i in (1, 2))
        logits = sb("logits", [P, B * C, E])
        biased = sb("biased", [P, B * C, E])
        rank_a, rank_b = (t[:].rearrange("p a s -> p (a s)").rearrange("p (t n) -> p t n", t=B * C)
                          for t in (d_sb, p_sb))
        rank = sb("rank", [P, B * C, E])
        probs = sb("probs", [P, B * C, E])
        total = sb("total", [P, B * C])
        weight = sb("weight", [P, B * C, NE])

        bank = [es.enter_context(nc.psum_tensor(f"bank{i}", [P, 512], F32)) for i in range(8)]

        l_x = [sem(f"l_x{b}") for b in range(B)]
        l_kT = [sem(f"l_kT{b}") for b in range(B)]
        l_ctx = [sem(f"l_ctx{b}") for b in range(B)]
        l_w = [sem(f"l_w{i}") for i in range(3)]
        l_gate, l_bias, l_consts, l_route = sem("l_gate"), sem("l_bias"), sem("l_consts"), sem("l_route")
        stored = sem("stored")
        g_step = sem("g_step")
        ident_ok, ident_b_ok, const_ok, ones_ok = sem("ident_ok"), sem("ident_b_ok"), sem("const_ok"), sem("ones_ok")
        before_ok = sem("before_ok")
        tanh_ok, gain_ok = sem("tanh_ok"), sem("gain_ok")
        pad_ok = sem("pad_ok")
        v_step = sem("v_step")
        mv1_ok, var1_ok, rs1_ok, q_ok, qT_psum, qT_ok = (sem(n) for n in ("mv1_ok", "var1_ok", "rs1_ok", "q_ok", "qT_psum", "qT_ok"))
        gates_ok, f_abs_ok, f_exp_ok, f_log_ok, a_ok, r1_ok, mid_ok, am3_ok = (
            sem(n) for n in ("gates_ok", "f_abs_ok", "f_exp_ok", "f_log_ok", "a_ok", "r1_ok", "mid_ok", "am3_ok"))
        m_ok, state_row_ok, rows_ok, rows_psum, ex_ok = (sem(n) for n in ("m_ok", "state_row_ok", "rows_ok", "rows_psum", "ex_ok"))
        decay_row_ok, decay_exp_ok, decay_psum, decay_ok = (sem(n) for n in ("decay_row_ok", "decay_exp_ok", "decay_psum", "decay_ok"))
        vaug_ok = sem("vaug_ok")
        kq_ok, k_wt_ok, d_ok, exp_ok, qk_ok, p_ok, pv_ok, pv_all = (
            sem(n) for n in ("kq_ok", "k_wt_ok", "d_ok", "exp_ok", "qk_ok", "p_ok", "pv_ok", "pv_all"))
        local_ok, masked_ok, carry_ok, state_ok, inter_ok, scaled_ok, comb_ok = (
            sem(n) for n in ("local_ok", "masked_ok", "carry_ok", "state_ok", "inter_ok", "scaled_ok", "comb_ok"))
        n0_ok, n1_ok, n2_ok, n3_ok, hn_ok, stA_ok, mvA_ok, varA_ok, rsA_ok, hl_ok, gained_ok, x1_ok = (
            sem(n) for n in ("n0_ok", "n1_ok", "n2_ok", "n3_ok", "hn_ok", "stA_ok", "mvA_ok", "varA_ok", "rsA_ok", "hl_ok", "gained_ok", "x1_ok"))
        stB_ok, mvB_ok, varB_ok, rsB_ok, xn_ok = (sem(n) for n in ("stB_ok", "mvB_ok", "varB_ok", "rsB_ok", "xn_ok"))
        w_hi_ok, w_ok = sem("w_hi_ok"), sem("w_ok")
        xT_psum, xT_hi_ok, xT_f_ok, xT_lo_ok = sem("xT_psum"), sem("xT_hi_ok"), sem("xT_f_ok"), sem("xT_lo_ok")
        logit_psum, logit_ok, r_step, sel_exp_ok, weight_ok = (
            sem(n) for n in ("logit_psum", "logit_ok", "r_step", "sel_exp_ok", "weight_ok"))
        up_ok, relu_ok, hi_ok, sq_ok, lo_ok, down_ok, acc_ok = (
            sem(n) for n in ("up_ok", "relu_ok", "hi_ok", "sq_ok", "lo_ok", "down_ok", "acc_ok"))

        block = es.enter_context(nc.Block())

        @block.sync
        def _(sp):
            sp.dma_start(x_all[:, 0], x[0].rearrange("(c p) d -> p c d", p=P)).then_inc(l_x[0], 16)
            sp.dma_start(gate_raw[:], gate_w.rearrange("p j (g h) -> p j g h", g=2)).then_inc(l_gate, 16)
            sp.dma_start(gate_bias[:], gate_b).then_inc(l_bias, 16)
            sp.dma_start(consts[:], row.to_broadcast([P, D + E + 2])).then_inc(l_consts, 16)
            sp.dma_start(kT_all[:, 0], ctxT[0].rearrange("(k p) s -> p k s", p=P)).then_inc(l_kT[0], 16)
            for b in range(1, B):
                sp.dma_start(x_all[:, b], x[b].rearrange("(c p) d -> p c d", p=P)).then_inc(l_x[b], 16)
                sp.dma_start(kT_all[:, b], ctxT[b].rearrange("(k p) s -> p k s", p=P)).then_inc(l_kT[b], 16)
            for b in range(B):
                sp.dma_start(ctx_all[:, b], ctx[b].rearrange("(c p) d -> p c d", p=P)).then_inc(l_ctx[b], 16)
            sp.dma_start(route[:], route_w).then_inc(l_route, 16)
            for e in range(NE):
                if e >= 3:
                    sp.wait_ge(w_ok, e - 2)
                    sp.wait_ge(w_hi_ok, e - 2)
                sp.dma_start(w_stage[:, e % 3], experts[:, e]).then_inc(l_w[e % 3], 16)
            for b in range(B):
                sp.wait_ge(acc_ok, (NE - 1) * B + b + 1)
                sp.dma_start(out[b].rearrange("(c p) d -> p c d", p=P), x_all[:, b]).then_inc(stored, 16)
            sp.wait_ge(stored, 16 * B)

        @block.gpsimd
        def _(gp):
            g = nc.gpsimd
            g.memset(ident[:], 0.0).then_inc(g_step, 1)
            gp.wait_ge(g_step, 1)
            g.affine_select(out=ident[:], in_=ident[:], compare_op=ALU.not_equal, fill=1.0, base=0,
                            pattern=[[-1, P]], channel_multiplier=1).then_inc(ident_ok, 1)
            g.memset(eps_c[:], LN_EPS)
            g.memset(neg_half[:], -0.5).then_inc(g_step, 1)
            gp.wait_ge(g_step, 2)

            def rsqrt(mv, rs, var_ok, n, done):
                g.tensor_tensor(mv[:, :, 1], mv[:, :, 1], eps_c[:], ALU.add).then_inc(var_ok, 1)
                gp.wait_ge(var_ok, n)
                g.tensor_tensor(rs, mv[:, :, 1], neg_half[:], ALU.pow).then_inc(done, 1)

            g.memset(gate_pad[:], 0.0).then_inc(g_step, 1)
            gp.wait_ge(l_gate, 16)
            g.tensor_copy(gate_sum[:, 0:KC], gate_raw[:, 0:KC])
            g.tensor_add(gate_sum[:, KC:], gate_raw[:, KC:2 * KC], gate_raw[:, 2 * KC:]).then_inc(g_step, 1)
            gp.wait_ge(g_step, 4)
            for b in range(B):
                for gate in range(2):
                    at = gate * NBH + b * NH
                    last = g.tensor_copy(gate_pad[:, b, :, at:at + NH], gate_sum[:, :, gate, :])
            last.then_inc(pad_ok, 1)
            for b in range(B):
                gp.wait_ge(mv1_ok, b + 1)
                rsqrt(mv1[:, b % 2], rs1[:, b % 2], var1_ok, b + 1, rs1_ok)
                if b == 0:
                    g.memset(ones_row[:], 1.0).then_inc(ones_ok, 1)
                    g.memset(zeros_c[:], 0.0).then_inc(g_step, 1)
                    g.memset(pick_small[:], 0.0).then_inc(g_step, 1)
                if b == 1:
                    gp.wait_ge(g_step, 6)
                    g.affine_select(out=mask[:], in_=zeros_c[:].rearrange("p (c s) -> p c s", c=C),
                                    compare_op=ALU.is_ge, fill=NEG, base=0,
                                    pattern=[[0, C], [1, P]], channel_multiplier=-1).then_inc(const_ok, 1)
                    g.tensor_copy(ident_b[:], ident[:]).then_inc(const_ok, 1)
            for q in range(3):
                g.affine_select(out=pick_small[:], in_=pick_small[:], compare_op=ALU.not_equal, fill=1.0,
                                base=-NBH * q, pattern=[[-1, NBH]], channel_multiplier=1).then_inc(g_step, 1)
                gp.wait_ge(g_step, 7 + q)
            g.tensor_copy(pick3[:], pick_small[:].unsqueeze(2).to_broadcast([96, NBH, P])).then_inc(const_ok, 1)
            g.tensor_copy(spread[:].rearrange("r g (h d) -> r (g h) d", h=4),
                          ident[0:NBH, 0:NBH].unsqueeze(2).to_broadcast([NBH, NBH, DH])).then_inc(const_ok, 1)
            g.memset(block_mask[:], SCALE).then_inc(g_step, 1)
            gp.wait_ge(g_step, 10)
            blocks = block_mask[:].rearrange("p (h d) -> p h d", h=4)
            g.affine_select(out=blocks, in_=blocks, compare_op=ALU.is_ge, fill=0.0, base=0,
                            pattern=[[-DH, 4], [0, DV]], channel_multiplier=1).then_inc(g_step, 1)
            gp.wait_ge(g_step, 11)
            g.affine_select(out=blocks, in_=blocks, compare_op=ALU.is_ge, fill=0.0, base=DH - 1,
                            pattern=[[DH, 4], [0, DV]], channel_multiplier=-1).then_inc(const_ok, 1)
            g.memset(vaug[:, :, :, :, DH:DV].rearrange("p b c h o -> p (b c h) o"), 1.0).then_inc(vaug_ok, 1)
            gp.wait_ge(m_ok, 1)
            g.tensor_tensor(rows[0:32].rearrange("p (c s) -> p c s", c=C),
                            am[:, 0].rearrange("p (c s) -> p c s", c=C),
                            am[:, 1].rearrange("p (c s) -> p c s", c=C)[:, :, P - 1:P].to_broadcast([NBH, C, P]),
                            ALU.add).then_inc(state_row_ok, 1)

            def work_copies(b):
                if not isinstance(b, int) or b > 0:
                    gp.wait_ge(qk_ok, b * NH)
                    gp.wait_ge(inter_ok, b * HG)
                g.tensor_copy(kT[:].rearrange("p k s -> p (k s)"),
                              kT_all[:, b].rearrange("p k s -> p (k s)")).then_inc(kq_ok, 1)
                g.tensor_copy(qT[:].rearrange("p k s -> p (k s)"),
                              qT_all[:, b].rearrange("p k s -> p (k s)")).then_inc(kq_ok, 1)

            def weigh_keys(b):
                if not isinstance(b, int) or b > 0:
                    gp.wait_ge(local_ok, b * HG)
                g.tensor_tensor(k_wt[:].rearrange("p c (h d) -> p c h d", h=NH),
                                vaug[:, b, 0:C - 1, :, 0:DH],
                                ex[:, 0:C - 1, bass.ds(b * NH, NH)].unsqueeze(3).to_broadcast([P, C - 1, NH, DH]),
                                ALU.mult).then_inc(k_wt_ok, 1)

            def attention_norm(t):
                gp.wait_ge(mvA_ok, t + 1)
                rsqrt(mv2, rs2[:], varA_ok, t + 1, rsA_ok)

            def add_residual(t):
                gp.wait_ge(hl_ok, t + 1)
                g.tensor_tensor(h_n[:], h_n[:], ln_gain[:].unsqueeze(1).to_broadcast([P, C, D]),
                                ALU.mult).then_inc(gained_ok, 1)
                gp.wait_ge(gained_ok, t + 1)
                g.tensor_tensor(x_all[:, t].rearrange("p c d -> p (c d)"),
                                x_all[:, t].rearrange("p c d -> p (c d)"),
                                h_n[:].rearrange("p c d -> p (c d)"), ALU.add).then_inc(x1_ok, 1)

            def expert_norm(t):
                gp.wait_ge(mvB_ok, t + 1)
                rsqrt(mv2, rs2[:], varB_ok, t + 1, rsB_ok)

            def low_part(b, i):
                e = 3 * (b - 1) + i
                gp.wait_ge(w_hi_ok, e + 1)
                g.tensor_tensor(w_lo[:, e].rearrange("p a k d -> p (a k d)"),
                                w_stage[:, i].rearrange("p a k d -> p (a k d)"),
                                w_hi[:, e].rearrange("p a k d -> p (a k d)"), ALU.subtract).then_inc(w_ok, 1)

            gp.wait_ge(l_kT[0], 16)
            gp.wait_ge(qT_ok, KC)
            work_copies(0)
            gp.wait_ge(vaug_ok, 1)
            for b in range(B):
                gp.wait_ge(l_ctx[b], 16)
                g.tensor_copy(vaug[:, b, :, :, 0:DH].rearrange("p c h d -> p (c h) d"),
                              ctx_all[:, b].rearrange("p c (h d) -> p (c h) d", h=NH)).then_inc(vaug_ok, 1)
                if b == 0:
                    gp.wait_ge(ex_ok, 1)
                    gp.wait_ge(vaug_ok, 2)
                    weigh_keys(0)
            g.memset(before[:], 1.0).then_inc(g_step, 1)
            gp.wait_ge(g_step, 12)
            g.affine_select(out=before[:], in_=before[:], compare_op=ALU.is_gt, fill=0.0, base=0,
                            pattern=[[1, E], [-1, E]], channel_multiplier=0).then_inc(before_ok, 1)
            gp.wait_ge(gain_ok, 1)
            gp.wait_ge(am3_ok, 1)
            gp.wait_ge(mid_ok, 1)
            gp.wait_ge(vaug_ok, 1 + B)
            gp.wait_ge(qT_ok, KC * B)
            for b in range(1, B):
                gp.wait_ge(l_kT[b], 16)
            with gp.Fori(1, B) as b:
                work_copies(b)
                weigh_keys(b)
                attention_norm(b - 1)
                low_part(b, 0)
                add_residual(b - 1)
                low_part(b, 1)
                expert_norm(b - 1)
                low_part(b, 2)
            attention_norm(B - 1)
            add_residual(B - 1)
            expert_norm(B - 1)

        @block.tensor
        def _(pe):
            mm = nc.tensor.matmul

            def transpose_q(b):
                if b >= 2:
                    pe.wait_ge(qT_ok, KC * (b - 1))
                pe.wait_ge(q_ok, b + 1)
                for k in range(KC):
                    for c in range(C):
                        last = nc.tensor.transpose(bank[2 + 2 * (b % 2) + k][:, c * P:(c + 1) * P],
                                                   q_tok[:, b % 2, c, k * P:(k + 1) * P], ident[:])
                    last.then_inc(qT_psum, 1)

            def gates_q(b):
                for k in range(KC):
                    pe.wait_ge(qT_ok, KC * b + k + 1)
                    last = mm(bank[0][0:2 * NBH, :], gate_pad[:, b, k, :], qT_all[:, b, k, :],
                              start=(b == 0 and k == 0), stop=(b == B - 1 and k == KC - 1))
                return last

            def gates_ctx(b):
                pe.wait_ge(l_kT[b], 16)
                for k in range(KC):
                    mm(bank[0][0:2 * NBH, :], gate_pad[:, b, KC + k, :], kT_all[:, b, k, :], start=False, stop=False)

            pe.wait_ge(ident_ok, 1)
            transpose_q(0)
            pe.wait_ge(pad_ok, 1)
            for b in range(B):
                if b + 1 < B:
                    if b == 0:
                        gates_q(0)
                        gates_ctx(0)
                        transpose_q(1)
                    else:
                        transpose_q(b + 1)
                        gates_ctx(b)
                        gates_q(b)
                else:
                    gates_ctx(b)
                    gates_q(b).then_inc(gates_ok, 1)

            def pairs(j, n):
                hg, r = j // 4, (j % 4) * DH
                return hg, r

            def head_scores(b, j):
                n = b * NH + j
                free = not isinstance(b, int) or n >= 2
                if free:
                    pe.wait_ge(exp_ok, n - 1)
                mm(bank[j % 2][:], pick3[:, n, :], am3[:, 1, :], start=True, stop=False)
                for c in range(C):
                    mm(bank[j % 2][:, c * P:(c + 1) * P], am3[:, 0, c * P:(c + 1) * P], pick3[:, n, :],
                       start=False, stop=False)
                mm(bank[j % 2][:], ident_b[:], mask[:].rearrange("p c s -> p (c s)"),
                   start=False, stop=True).then_inc(d_ok, 1)
                if j == 0:
                    pe.wait_ge(kq_ok, 2 * b + 2)
                if free:
                    pe.wait_ge(p_ok, n - 1)
                hg, r = j // 4, (j % 4) * DH
                for c in range(C):
                    last = mm(bank[2 + j % 2][:, c * P:(c + 1) * P], kT[r:r + DH, hg, c * P:(c + 1) * P],
                              qT[r:r + DH, hg, c * P:(c + 1) * P], start=True, stop=True)
                last.then_inc(qk_ok, 1)

            def head_values(b, j):
                n = b * NH + j
                pe.wait_ge(p_ok, n + 1)
                if j % 4 == 0 and (not isinstance(b, int) or n > 0):
                    pe.wait_ge(comb_ok, b * HG + j // 4)
                for c in range(C):
                    at = (c % 2) * GV + (j % 4) * DV
                    last = mm(bank[4 + c // 2][:, at:at + DV], p_sb[:, j % 2, c * P:(c + 1) * P],
                              vaug[:, b, c, j, :], start=True, stop=True)
                last.then_inc(pv_ok, 1)

            def group_state(b, hg):
                if hg == 0:
                    pe.wait_ge(k_wt_ok, b + 1)
                if not isinstance(b, int) or b + hg > 0:
                    pe.wait_ge(masked_ok, b * HG + hg)
                for c in range(C - 1):
                    last = mm(bank[7][:, c * GV:(c + 1) * GV], k_wt[:, c, hg * P:(hg + 1) * P],
                              vaug[:, b, c, hg * 4:hg * 4 + 4, :].rearrange("p h d -> p (h d)"), start=True, stop=True)
                last.then_inc(local_ok, 1)

            def group_inter(b, hg):
                pe.wait_ge(state_ok, b * HG + hg + 1)
                if not isinstance(b, int) or b + hg > 0:
                    pe.wait_ge(comb_ok, b * HG + hg)
                for c in range(1, C):
                    last = mm(bank[6][:, (c - 1) * GV:c * GV], qT[:, hg, c * P:(c + 1) * P],
                              state[:, hg, c - 1, :], start=True, stop=True)
                last.then_inc(inter_ok, 1)

            def batch(b):
                for j in range(NH):
                    head_scores(b, j)
                    if j % 4 == 0:
                        group_state(b, j // 4)
                    if j > 0:
                        head_values(b, j - 1)
                    if j % 4 == 3:
                        group_inter(b, j // 4)
                head_values(b, NH - 1)

            pe.wait_ge(const_ok, 5)
            pe.wait_ge(rows_ok, 1)
            pe.wait_ge(state_row_ok, 1)
            for c in range(C):
                last = nc.tensor.transpose(bank[1][:, c * 96:(c + 1) * 96], rows[:, c * P:(c + 1) * P],
                                           ident[0:96, 0:96])
            last.then_inc(rows_psum, 1)
            pe.wait_ge(decay_exp_ok, 1)
            for n in range(B * HG):
                last = mm(bank[0][:, 2 * n:2 * n + 2], spread[:, n, :], decay_exp[:], start=True, stop=True)
            last.then_inc(decay_psum, 1)
            pe.wait_ge(am3_ok, 1)
            pe.wait_ge(mid_ok, 1)
            pe.wait_ge(ex_ok, 1)
            pe.wait_ge(decay_ok, 1)
            pe.wait_ge(vaug_ok, 2)
            batch(0)
            pe.wait_ge(vaug_ok, 1 + B)
            with pe.Fori(1, B) as b:
                batch(b)

            def transpose_x(b, lo):
                pe.wait_ge(xn_ok, b + 1)
                for k in range(KC):
                    for c in range(C):
                        last = nc.tensor.transpose(bank[lo + k][:, c * P:(c + 1) * P],
                                                   xn[:, b, c, k * P:(k + 1) * P], ident[:])
                    last.then_inc(xT_psum, 1)

            def router(b, to, at):
                pe.wait_ge(xT_f_ok, KC * (b + 1))
                for c in range(C):
                    for k in range(KC):
                        last = mm(to[:, at + c * E:at + (c + 1) * E], xT[:, b, k, c * P:(c + 1) * P], route[:, k, :],
                                  start=(k == 0), stop=(k == KC - 1))
                last.then_inc(logit_psum, 1)

            def up(e, b):
                n = e * B + b
                if b == 0:
                    pe.wait_ge(w_ok, e + 1)
                if not isinstance(n, int) or n >= 2:
                    pe.wait_ge(relu_ok, KC * (n - 1))
                for h in range(KC):
                    for k in range(KC):
                        for m, (w, xx) in enumerate(((w_hi, xT_hi), (w_hi, xT_lo), (w_lo, xT_hi))):
                            last = mm(bank[2 * (b % 2) + h][:], w[:, e, 0, k, h * P:(h + 1) * P], xx[:, b, k, :],
                                      start=(k == 0 and m == 0), stop=(k == KC - 1 and m == MIXED - 1))
                    last.then_inc(up_ok, 1)

            def down(e, b):
                n = e * B + b
                pe.wait_ge(hi_ok, KC * (n + 1))
                pe.wait_ge(lo_ok, KC * (n + 1))
                if not isinstance(n, int) or n >= 2:
                    pe.wait_ge(acc_ok, n - 1)
                for c in range(C):
                    for h in range(KC):
                        for m, (s, w) in enumerate(((sq_hi, w_hi), (sq_hi, w_lo), (sq_lo, w_hi))):
                            at = (c % 2) * D
                            last = mm(bank[4 + 2 * (b % 2) + c // 2][:, at:at + D],
                                      s[:, b % 2, h, c * P:(c + 1) * P], w[:, e, 1, h, :],
                                      start=(h == 0 and m == 0), stop=(h == KC - 1 and m == MIXED - 1))
                last.then_inc(down_ok, 1)

            pe.wait_ge(comb_ok, HG * B)
            pe.wait_ge(l_route, 16)
            transpose_x(0, 4)
            transpose_x(1, 6)
            transpose_x(2, 0)
            pe.wait_ge(xT_lo_ok, KC * 3)
            pe.wait_ge(xT_f_ok, KC * 3)
            pe.wait_ge(xT_hi_ok, KC * 3)
            for b in range(3):
                router(b, bank[2], b * C * E)
            up(0, 0)
            pe.wait_ge(logit_ok, 1)
            up(0, 1)
            down(0, 0)
            transpose_x(3, 6)
            pe.wait_ge(xT_lo_ok, KC * 4)
            pe.wait_ge(xT_hi_ok, KC * 4)
            router(3, bank[6], 0)
            up(0, 2)
            pe.wait_ge(logit_ok, 2)
            down(0, 1)
            up(0, 3)
            down(0, 2)
            with pe.Fori(1, NE) as e:
                up(e, 0)
                down(e - 1, B - 1)
                for b in range(1, B):
                    up(e, b)
                    down(e, b - 1)
            down(NE - 1, B - 1)

        @block.scalar
        def _(act):
            s = nc.scalar
            act.wait_ge(l_consts, 16)
            s.activation(tanhs[:], consts[:, D + E:D + E + 2], ACT.Tanh).then_inc(tanh_ok, 1)
            for b in range(B):
                for k in range(KC):
                    act.wait_ge(qT_psum, KC * b + k + 1)
                    s.activation(qT_all[:, b, k, :], bank[2 + 2 * (b % 2) + k][:], ACT.Copy).then_inc(qT_ok, 1)
            act.wait_ge(f_abs_ok, 1)
            s.activation(f_abs, f_abs, ACT.Exp, scale=-1.0).then_inc(f_exp_ok, 1)
            act.wait_ge(f_exp_ok, 1)
            s.activation(f_abs, f_abs, ACT.Ln, bias=1.0).then_inc(f_log_ok, 1)
            act.wait_ge(r1_ok, 1)
            s.activation(am3[32:64], am_rest, ACT.Copy).then_inc(mid_ok, 1)
            act.wait_ge(decay_row_ok, 1)
            s.activation(decay_exp[:], decay_row[:], ACT.Exp).then_inc(decay_exp_ok, 1)
            act.wait_ge(rows_psum, 1)
            s.activation(ex[:].rearrange("p c r -> p (c r)"), bank[1][:, 0:C * 96], ACT.Exp).then_inc(ex_ok, 1)
            act.wait_ge(decay_psum, 1)
            s.activation(decay[:].rearrange("p n t -> p (n t)"), bank[0][:, 0:4 * B], ACT.Copy).then_inc(decay_ok, 1)

            def head_exp(b, j):
                n = b * NH + j
                act.wait_ge(d_ok, n + 1)
                if not isinstance(b, int) or n >= 2:
                    act.wait_ge(p_ok, n - 1)
                s.activation(d_sb[:, j % 2, :], bank[j % 2][:], ACT.Exp).then_inc(exp_ok, 1)

            def high_part(b, i):
                e = 3 * (b - 1) + i
                act.wait_ge(l_w[i], 16 * b)
                s.activation(w_hi[:, e].rearrange("p a k d -> p (a k d)"),
                             w_stage[:, i].rearrange("p a k d -> p (a k d)"), ACT.Copy).then_inc(w_hi_ok, 1)

            for j in range(NH):
                head_exp(0, j)
            with act.Fori(1, B) as b:
                for j in range(NH):
                    head_exp(b, j)
                    if j % 2 == 1 and j < 6:
                        high_part(b, j // 2)

            def copy_x(b, lo):
                for k in range(KC):
                    act.wait_ge(xT_psum, KC * b + k + 1)
                    s.activation(xT_hi[:, b, k, :], bank[lo + k][:], ACT.Copy).then_inc(xT_hi_ok, 1)
                    s.activation(xT[:, b, k, :], bank[lo + k][:], ACT.Copy).then_inc(xT_f_ok, 1)

            def relu(e, b):
                n = e * B + b
                for h in range(KC):
                    act.wait_ge(up_ok, KC * n + h + 1)
                    if not isinstance(n, int) or n >= 2:
                        act.wait_ge(sq_ok, KC * (n - 2) + h + 1)
                    s.activation(relu_z[:, b % 2, h, :], bank[2 * (b % 2) + h][:], ACT.Relu).then_inc(relu_ok, 1)
                for h in range(KC):
                    act.wait_ge(relu_ok, KC * n + h + 1)
                    if not isinstance(n, int) or n >= 2:
                        act.wait_ge(down_ok, n - 1)
                    s.activation(sq_hi[:, b % 2, h, :], relu_z[:, b % 2, h, :], ACT.Square).then_inc(hi_ok, 1)

            copy_x(0, 4)
            copy_x(1, 6)
            copy_x(2, 0)
            act.wait_ge(logit_psum, 3)
            s.activation(logits[:, 0:3 * C].rearrange("p t e -> p (t e)"), bank[2][:, 0:3 * C * E],
                         ACT.Copy).then_inc(logit_ok, 1)
            relu(0, 0)
            relu(0, 1)
            copy_x(3, 6)
            act.wait_ge(logit_psum, 4)
            s.activation(logits[:, 3 * C:].rearrange("p t e -> p (t e)"), bank[6][:, 0:C * E],
                         ACT.Copy).then_inc(logit_ok, 1)
            act.wait_ge(logit_ok, 2)
            s.activation(probs[:], logits[:], ACT.Exp, scale=-1.0).then_inc(sel_exp_ok, 1)
            relu(0, 2)
            relu(0, 3)
            with act.Fori(1, NE) as e:
                for b in range(B):
                    relu(e, b)

        @block.vector
        def _(dve):
            v = nc.vector
            steps = [0]

            def step(ins):
                steps[0] += 1
                ins.then_inc(v_step, 1)
                dve.wait_ge(v_step, steps[0])

            def stats(b):
                dve.wait_ge(l_x[b], 16)
                if b >= 2:
                    dve.wait_ge(rs1_ok, b - 1)
                for c in range(C):
                    last = v.bn_stats(st1[:, b % 2, c, :], x_all[:, b, c, :])
                step(last)
                for c in range(C):
                    last = v.bn_aggr(mv1[:, b % 2, c, :], st1[:, b % 2, c, :])
                last.then_inc(mv1_ok, 1)

            def normalise(b):
                dve.wait_ge(rs1_ok, b + 1)
                if b >= 2:
                    dve.wait_ge(qT_psum, KC * (b - 1))
                for c in range(C):
                    last = v.tensor_scalar(q_tok[:, b % 2, c, :], x_all[:, b, c, :], mv1[:, b % 2, c, 0:1],
                                           rs1[:, b % 2, c:c + 1], ALU.subtract, ALU.mult)
                last.then_inc(q_ok, 1)

            step(v.memset(rows[32:64, 0:P], 0.0))
            stats(0)
            for b in range(B):
                if b + 1 < B:
                    stats(b + 1)
                normalise(b)
            dve.wait_ge(tanh_ok, 1)
            v.tensor_scalar(ln_gain[:], consts[:, 0:D], tanhs[:, 0:1], None, ALU.mult).then_inc(gain_ok, 1)

            dve.wait_ge(gates_ok, 1)
            dve.wait_ge(l_bias, 16)
            step(v.tensor_scalar(f_pre, bank[0][NBH:2 * NBH, :], gate_bias[:, 1:2], None, ALU.add))
            v.scalar_tensor_tensor(f_abs, f_pre, -1.0, f_pre, ALU.mult, ALU.max).then_inc(f_abs_ok, 1)
            dve.wait_ge(f_log_ok, 1)
            step(v.scalar_tensor_tensor(log_f, f_pre, 0.0, f_abs, ALU.min, ALU.subtract))
            dve.wait_ge(ones_ok, 1)
            step(v.tensor_tensor_scan(cs, log_f, ones_row[:], 0.0, ALU.add, ALU.mult))
            step(v.scalar_tensor_tensor(am[:, 0], bank[0][0:NBH, :], gate_bias[:, 0:1], cs,
                                        ALU.add, ALU.subtract))
            step(v.tensor_tensor_scan(f_pre, am[:, 0], am[:, 0], LOWEST, ALU.max, ALU.max))
            step(v.tensor_scalar(am[:, 1], f_pre, -1.0, None, ALU.mult))
            m_row = f_pre
            m_end = f_pre.rearrange("p (c s) -> p c s", c=C)[:, :, P - 1:P]
            v.tensor_copy(am3[0:32], am).then_inc(m_ok, 1)
            v.tensor_tensor(decay_row[:].unsqueeze(2), m_end[:, 0:2], m_end[:, 1:3], ALU.subtract)\
                .then_inc(decay_row_ok, 1)
            dve.wait_ge(m_ok, 1)
            v.tensor_tensor(am_rest, am, am3[0:32], ALU.subtract).then_inc(r1_ok, 1)
            v.tensor_tensor(rows[32:64, P:].rearrange("p (c s) -> p c s", c=C - 1),
                            m_end[:, 0:C - 1].to_broadcast([NBH, C - 1, P]),
                            m_row[:, P:].rearrange("p (c s) -> p c s", c=C - 1), ALU.subtract)
            v.scalar_tensor_tensor(rows[64:96], cs, -1.0, m_row[:], ALU.mult, ALU.subtract).then_inc(rows_ok, 1)
            dve.wait_ge(r1_ok, 1)
            step(v.tensor_copy(am_mid, am_rest))
            v.tensor_tensor(am3[64:96], am_rest, am_mid, ALU.subtract).then_inc(am3_ok, 1)

            def head_product(b, j):
                n = b * NH + j
                dve.wait_ge(exp_ok, n + 1)
                dve.wait_ge(qk_ok, n + 1)
                if not isinstance(b, int) or n >= 2:
                    dve.wait_ge(pv_ok, n - 1)
                v.scalar_tensor_tensor(p_sb[:, j % 2, :], bank[2 + j % 2][:], SCALE, d_sb[:, j % 2, :],
                                       ALU.mult, ALU.mult).then_inc(p_ok, 1)

            def group_states(b, hg):
                n = b * HG + hg
                dve.wait_ge(local_ok, n + 1)
                if not isinstance(b, int) or b > 0:
                    dve.wait_ge(inter_ok, n - 1)
                v.tensor_tensor(state[:, hg], bank[7][:, 0:(C - 1) * GV].rearrange("p (c g) -> p c g", c=C - 1),
                                block_mask[:].unsqueeze(1).to_broadcast([P, C - 1, GV]), ALU.mult).then_inc(masked_ok, 1)
                dve.wait_ge(masked_ok, n + 1)
                v.scalar_tensor_tensor(state[:, hg, 1], state[:, hg, 0], decay[:, n, 0:1], state[:, hg, 1],
                                       ALU.mult, ALU.add).then_inc(carry_ok, 1)
                dve.wait_ge(carry_ok, n + 1)
                v.scalar_tensor_tensor(state[:, hg, 2], state[:, hg, 1], decay[:, n, 1:2], state[:, hg, 2],
                                       ALU.mult, ALU.add).then_inc(state_ok, 1)

            def group_combine(b, hg):
                n = b * HG + hg
                dve.wait_ge(inter_ok, n + 1)
                v.tensor_tensor(carried[:].rearrange("p c (h d) -> p c h d", h=4),
                                bank[6][:, 0:(C - 1) * GV].rearrange("p (c h d) -> p c h d", c=C - 1, h=4),
                                ex[:, 1:C, bass.ds(NBH + n * 4, 4)].unsqueeze(3).to_broadcast([P, C - 1, 4, DV]),
                                ALU.mult).then_inc(scaled_ok, 1)
                dve.wait_ge(pv_ok, (n + 1) * 4)
                h4 = h_sum[:, :, hg * 4:hg * 4 + 4, :].rearrange("p c h d -> p c (h d)")
                v.tensor_copy(h4[:, 0], bank[4][:, 0:GV])
                dve.wait_ge(scaled_ok, n + 1)
                v.tensor_tensor(h4[:, 1], bank[4][:, GV:2 * GV], carried[:, 0], ALU.add)
                v.tensor_tensor(h4[:, 2:4], bank[5][:, 0:2 * GV].rearrange("p (c g) -> p c g", c=2),
                                carried[:, 1:3], ALU.add).then_inc(comb_ok, 1)

            def norm_max(t):
                dve.wait_ge(comb_ok, HG * (t + 1))
                v.scalar_tensor_tensor(norm[:, 0], h_sum[:, :, :, DH], -1.0, ex[:, :, bass.ds(2 * NBH + t * NH, NH)],
                                       ALU.mult, ALU.max).then_inc(n0_ok, 1)

            def norm_eps(t):
                dve.wait_ge(n0_ok, t + 1)
                v.tensor_tensor(norm[:, 2], norm[:, 0], h_sum[:, :, :, DH], ALU.max).then_inc(n1_ok, 1)
                dve.wait_ge(n1_ok, t + 1)
                v.tensor_scalar(norm[:, 1], norm[:, 2], EPS, None, ALU.add).then_inc(n2_ok, 1)

            def norm_divide(t):
                dve.wait_ge(n2_ok, t + 1)
                v.reciprocal(norm[:, 2], norm[:, 1]).then_inc(n3_ok, 1)
                dve.wait_ge(n3_ok, t + 1)
                v.tensor_tensor(h_n[:].rearrange("p c (h d) -> p (c h) d", h=NH),
                                h_sum[:, :, :, 0:DH].rearrange("p c h d -> p (c h) d"),
                                norm[:, 2].rearrange("p c h -> p (c h)").unsqueeze(2).to_broadcast([P, C * NH, DH]),
                                ALU.mult).then_inc(hn_ok, 1)

            def statsA(t):
                dve.wait_ge(hn_ok, t + 1)
                for c in range(C):
                    last = v.bn_stats(st2[:, c, :], h_n[:, c, :])
                last.then_inc(stA_ok, 1)

            def meanA(t):
                for c in range(C):
                    last = v.bn_aggr(mv2[:, c, :], st2[:, c, :])
                last.then_inc(mvA_ok, 1)

            def normaliseA(t):
                dve.wait_ge(rsA_ok, t + 1)
                for c in range(C):
                    last = v.tensor_scalar(h_n[:, c, :], h_n[:, c, :], mv2[:, c, 0:1], rs2[:, c:c + 1],
                                           ALU.subtract, ALU.mult)
                last.then_inc(hl_ok, 1)

            def statsB(t):
                dve.wait_ge(x1_ok, t + 1)
                for c in range(C):
                    last = v.bn_stats(st2[:, c, :], x_all[:, t, c, :])
                last.then_inc(stB_ok, 1)

            def meanB(t):
                for c in range(C):
                    last = v.bn_aggr(mv2[:, c, :], st2[:, c, :])
                last.then_inc(mvB_ok, 1)

            def normaliseB(t):
                dve.wait_ge(rsB_ok, t + 1)
                for c in range(C):
                    last = v.tensor_scalar(xn[:, t, c, :], x_all[:, t, c, :], mv2[:, c, 0:1], rs2[:, c:c + 1],
                                           ALU.subtract, ALU.mult)
                last.then_inc(xn_ok, 1)

            after_head = {0: norm_max, 1: norm_eps, 2: norm_divide, 3: statsA, 4: meanA, 5: normaliseA, 7: statsB}

            def batch(b, tail):
                for j in range(NH):
                    if tail and j == 4:
                        dve.wait_ge(stA_ok, b)
                    head_product(b, j)
                    if j % 4 == 0:
                        group_states(b, j // 4)
                    if tail and j in after_head:
                        after_head[j](b - 1)
                    if j == 5:
                        group_combine(b, 0)
                if tail:
                    dve.wait_ge(stB_ok, b)
                group_combine(b, 1)
                if tail:
                    meanB(b - 1)
                    normaliseB(b - 1)

            dve.wait_ge(decay_ok, 1)
            dve.wait_ge(const_ok, 5)
            dve.wait_ge(ex_ok, 1)
            batch(0, False)
            dve.wait_ge(vaug_ok, 1 + B)
            with dve.Fori(1, B) as b:
                batch(b, True)

            def low_x(b, lo):
                for k in range(KC):
                    dve.wait_ge(xT_f_ok, KC * b + k + 1)
                    v.tensor_tensor(xT_lo[:, b, k, :], bank[lo + k][:], xT_hi[:, b, k, :],
                                    ALU.subtract).then_inc(xT_lo_ok, 1)

            def square(e, b):
                n = e * B + b
                for h in range(KC):
                    dve.wait_ge(relu_ok, KC * n + h + 1)
                    if not isinstance(n, int) or n >= 1:
                        dve.wait_ge(lo_ok, KC * (n - 1) + h + 1)
                    v.tensor_tensor(sq[:, h, :], relu_z[:, b % 2, h, :], relu_z[:, b % 2, h, :],
                                    ALU.mult).then_inc(sq_ok, 1)
                for h in range(KC):
                    dve.wait_ge(sq_ok, KC * n + h + 1)
                    dve.wait_ge(hi_ok, KC * n + h + 1)
                    v.tensor_tensor(sq_lo[:, b % 2, h, :], sq[:, h, :], sq_hi[:, b % 2, h, :],
                                    ALU.subtract).then_inc(lo_ok, 1)

            def accumulate(e, b):
                n = e * B + b
                dve.wait_ge(down_ok, n + 1)
                if not isinstance(n, int) or n >= B:
                    dve.wait_ge(acc_ok, n - B + 1)
                for c in range(C):
                    at = (c % 2) * D
                    last = v.scalar_tensor_tensor(x_all[:, b, c, :], bank[4 + 2 * (b % 2) + c // 2][:, at:at + D],
                                                  weight[:, b * C + c, bass.ds(e, 1)], x_all[:, b, c, :],
                                                  ALU.mult, ALU.add)
                last.then_inc(acc_ok, 1)

            low_x(0, 4)
            low_x(1, 6)
            low_x(2, 0)
            norm_max(B - 1)
            norm_eps(B - 1)
            norm_divide(B - 1)
            statsA(B - 1)
            dve.wait_ge(stA_ok, B)
            meanA(B - 1)
            normaliseA(B - 1)
            v.tensor_copy(weight[:, :, 0], tanhs[:, 1:2].to_broadcast([P, B * C])).then_inc(r_step, 1)
            square(0, 0)
            statsB(B - 1)
            dve.wait_ge(stB_ok, B)
            meanB(B - 1)
            normaliseB(B - 1)
            dve.wait_ge(r_step, 1)
            square(0, 1)
            accumulate(0, 0)
            low_x(3, 6)
            dve.wait_ge(logit_ok, 2)
            v.tensor_tensor(biased[:], logits[:], consts[:, D:D + E].unsqueeze(1).to_broadcast([P, B * C, E]),
                            ALU.add).then_inc(r_step, 1)
            dve.wait_ge(r_step, 2)
            other = biased[:].unsqueeze(2).to_broadcast([P, B * C, E, E])
            own = biased[:].unsqueeze(3).to_broadcast([P, B * C, E, E])
            four = "p t (j i) -> p t j i"
            v.tensor_tensor(rank_a[:].rearrange(four, j=E), other, own, ALU.is_gt)
            v.tensor_tensor(rank_b[:].rearrange(four, j=E), other, own, ALU.is_equal).then_inc(r_step, 1)
            square(0, 2)
            accumulate(0, 1)
            dve.wait_ge(r_step, 3)
            dve.wait_ge(before_ok, 1)
            v.tensor_tensor(rank_b[:], rank_b[:], before[:].rearrange("p j i -> p (j i)").unsqueeze(1)
                            .to_broadcast([P, B * C, E * E]), ALU.mult).then_inc(r_step, 1)
            dve.wait_ge(r_step, 4)
            v.tensor_tensor(rank_a[:], rank_a[:], rank_b[:], ALU.add).then_inc(r_step, 1)
            dve.wait_ge(r_step, 5)
            v.tensor_reduce(rank[:], rank_a[:].rearrange(four, j=E), AX.X, ALU.add).then_inc(r_step, 1)
            dve.wait_ge(sel_exp_ok, 1)
            v.tensor_scalar(probs[:], probs[:], 1.0, None, ALU.add).then_inc(r_step, 1)
            dve.wait_ge(r_step, 7)
            v.reciprocal(probs[:], probs[:]).then_inc(r_step, 1)
            dve.wait_ge(r_step, 8)
            v.scalar_tensor_tensor(probs[:], rank[:], 1.5, probs[:], ALU.is_lt, ALU.mult).then_inc(r_step, 1)
            square(0, 3)
            accumulate(0, 2)
            dve.wait_ge(r_step, 9)
            v.tensor_reduce(total[:], probs[:], AX.X, ALU.add).then_inc(r_step, 1)
            dve.wait_ge(r_step, 10)
            v.tensor_scalar(total[:], total[:], W_EPS, None, ALU.add).then_inc(r_step, 1)
            dve.wait_ge(r_step, 11)
            v.reciprocal(total[:], total[:]).then_inc(r_step, 1)
            dve.wait_ge(r_step, 12)
            v.tensor_scalar(total[:], total[:], tanhs[:, 1:2], None, ALU.mult).then_inc(r_step, 1)
            dve.wait_ge(r_step, 13)
            v.tensor_tensor(weight[:, :, 1:NE], probs[:], total[:].unsqueeze(2).to_broadcast([P, B * C, E]),
                            ALU.mult).then_inc(weight_ok, 1)
            dve.wait_ge(weight_ok, 1)
            with dve.Fori(1, NE) as e:
                square(e, 0)
                accumulate(e - 1, B - 1)
                for b in range(1, B):
                    square(e, b)
                    accumulate(e, b - 1)
            accumulate(NE - 1, B - 1)


def kernel(x, ctx_1024, g_xattn, g_ffn, L0_xattn_igate_w, L0_xattn_igate_b, L0_xattn_fgate_w, L0_xattn_fgate_b,
           L0_xattn_ln_scale, L0_ffn_gate_w, L0_ffn_lb_bias, L0_ffn_w1, L0_ffn_w2, L0_ffn_cfc, L0_ffn_cproj):
    import concourse.bacc as bacc
    from concourse.bass_utils import run_bass_kernel_spmd

    a = np.asarray

    def halves(w):
        return a(w).transpose(2, 0, 1).reshape(KC, P, -1, w.shape[1]).transpose(1, 2, 0, 3)

    up = np.concatenate([halves(a(L0_ffn_cfc)[None]), halves(a(L0_ffn_w1))], 1)
    down = np.concatenate([halves(a(L0_ffn_cproj)[None]), halves(a(L0_ffn_w2))], 1)
    gates = np.concatenate([a(L0_xattn_igate_w), a(L0_xattn_fgate_w)], 0)
    arrays = {
        "x": a(x),
        "ctx": a(ctx_1024),
        "ctxT": a(ctx_1024).transpose(0, 2, 1),
        "experts": np.stack([up, down], 2),
        "gate_w": gates.T.reshape(3 * KC, P, 2 * NH).transpose(1, 0, 2),
        "gate_b": np.stack([np.tile(a(L0_xattn_igate_b), B), np.tile(a(L0_xattn_fgate_b), B)], 1),
        "row": np.concatenate([a(L0_xattn_ln_scale), a(L0_ffn_lb_bias), a(g_xattn), a(g_ffn)])[None],
        "route_w": a(L0_ffn_gate_w).T.reshape(KC, P, E).transpose(1, 0, 2),
    }
    arrays = {n: np.ascontiguousarray(v) for n, v in arrays.items()}
    nc = bacc.Bacc("TRN2", target_bir_lowering=False, num_devices=1)
    args = {n: nc.dram_tensor(n, v.shape, F32, kind="ExternalInput").ap() for n, v in arrays.items()}
    out = nc.dram_tensor("out", (B, S, D), F32, kind="ExternalOutput").ap()
    gated_block(nc, out=out, **args)
    r = run_bass_kernel_spmd(nc, [arrays], core_ids=[0])
    return r.results[0]["out"]
```

```python
from contextlib import ExitStack

import numpy as np
import concourse.bass as bass
from concourse import mybir

F32 = mybir.dt.float32
BF16 = mybir.dt.bfloat16
ALU = mybir.AluOpType
ACT = mybir.ActivationFunctionType
AX = mybir.AxisListType

P = 128
B, S, D = 4, 512, 256
NH, DH = 8, 32
C = S // P
KC = D // P
NBH = B * NH
HG = NH // 4
DV = DH + 1
GV = 4 * DV
E = 8
NE = E + 1
MIXED = 3
LN_EPS, EPS, W_EPS = 1e-5, 1e-6, 1e-6
SCALE = float(DH) ** -0.5
NEG = -1e30
LOWEST = -3.0e38


def gated_block(nc, x, ctx, ctxT, experts, gate_w, gate_b, row, route_w, out):
    es = ExitStack()
    with es:
        def sb(name, shape, dt=F32):
            return es.enter_context(nc.sbuf_tensor(name, shape, dt))

        def sem(name):
            return es.enter_context(nc.semaphore(name))

        x_all = sb("x_all", [P, B, C, D])
        qT2 = sb("qT2", [P, 2, B, KC, S], BF16)
        kT2 = sb("kT2", [P, 2, B, KC, S], BF16)
        q_pad = sb("q_pad", [P, 2, NH, S], BF16)
        xn = sb("xn", [P, B, C, D])
        vaug = sb("vaug", [P, B, C, NH, DV])
        w_hi = sb("w_hi", [P, NE, 2, KC, D], BF16)
        w_lo = sb("w_lo", [P, NE, 2, KC, D], BF16)
        w_stage = sb("w_stage", [P, 3, 2, KC, D])
        xT = qT2[:].rearrange("p t b k s -> p (t b k s)").bitcast(F32).rearrange("p (b k s) -> p b k s", b=B, k=KC)
        xT_hi, xT_lo = kT2[:, 0], kT2[:, 1]
        kT_stage = w_hi[:].rearrange("p e a k d -> p (e a k d)").bitcast(F32)[:, 0:B * KC * S]\
            .rearrange("p (b k s) -> p b k s", b=B, k=KC)
        ident = sb("ident", [P, P])
        ident_b = sb("ident_b", [P, P], BF16)
        mask = sb("mask", [P, C, P], BF16)
        zeros_c = sb("zeros_c", [P, C * P], BF16)
        pick3 = sb("pick3", [96, NBH], BF16)
        is_head = sb("is_head", [NBH, 4])
        head_rows = sb("head_rows", [NBH, P])
        is_group = sb("is_group", [NBH, B * HG])
        block_mask = sb("block_mask", [P, GV])
        neg_half = sb("neg_half", [P, C])
        eps_c = sb("eps_c", [P, C])
        ones_row = sb("ones_row", [NBH, S])
        before = sb("before", [P, E, E])
        consts = sb("consts", [P, D + E + 2])
        tanhs = sb("tanhs", [P, 2])
        ln_gain = sb("ln_gain", [P, D])
        gate_raw = sb("gate_raw", [P, 3 * KC, 2, NH])
        gate_sum = sb("gate_sum", [P, 2 * KC, 2, NH])
        gate_part = sb("gate_part", [P, 2, 2 * KC, 2 * NH], BF16)
        gate_pad = sb("gate_pad", [P, B, 2 * KC, 2, 2 * NBH], BF16)
        lo_rows = sb("lo_rows", [NBH, 2, S])
        gate_bias = sb("gate_bias", [NBH, 2])
        route = sb("route", [P, KC, E])
        scratch = w_lo[0:NBH].rearrange("p e a k d -> p (e a k d)").bitcast(F32)
        f_pre, f_abs, log_f, cs = (scratch[:, i * S:(i + 1) * S] for i in range(4))
        am = scratch[:, 4 * S:6 * S].rearrange("p (t s) -> p t s", t=2)
        am_rest = scratch[:, 6 * S:8 * S].rearrange("p (t s) -> p t s", t=2)
        am_mid = scratch[:, 8 * S:9 * S].bitcast(BF16).rearrange("p (t s) -> p t s", t=2)
        am3 = sb("am3", [96, 2, S], BF16)
        rows = sb("rows", [96, S])
        decay_row = sb("decay_row", [NBH, 2])
        decay_exp = sb("decay_exp", [NBH, 2])
        decay_wide = sb("decay_wide", [NBH, B * HG, 2])
        decay = sb("decay", [P, B * HG, 2])
        ex = sb("ex", [P, C, 96])
        st1 = sb("st1", [P, 2, C, 6])
        mv1 = sb("mv1", [P, 2, C, 2])
        rs1 = sb("rs1", [P, 2, C])
        nb1 = sb("nb1", [P, 2, C])
        q_tok = sb("q_tok", [P, 2, C, D])
        st2 = sb("st2", [P, C, 6])
        mv2 = sb("mv2", [P, C, 2])
        rs2 = sb("rs2", [P, C])
        nb2 = sb("nb2", [P, C])
        minus1 = sb("minus1", [P, C])
        k_wt = sb("k_wt", [P, C - 1, D])
        d_sb = sb("d_sb", [P, 2, S])
        p_sb = sb("p_sb", [P, 2, S])
        state = sb("state", [P, HG, C - 1, GV])
        state2 = sb("state2", [P, 2, HG, C - 1, GV], BF16)
        carried = sb("carried", [P, C - 1, GV])
        h_sum = sb("h_sum", [P, C, NH, DV])
        norm = sb("norm", [P, 3, C, NH])
        h_n = sb("h_n", [P, C, D])
        relu_z = q_tok[:, :, :, :].rearrange("p a c d -> p a (c d)").rearrange("p a (h s) -> p a h s", h=KC)
        values = vaug[:].rearrange("p b c h d -> p (b c h d)")
        sq = values[:, 0:KC * S].rearrange("p (h s) -> p h s", h=KC)
        sq_hi, sq_lo = (values[:, i * KC * S:(i + 1) * KC * S].bitcast(BF16)
                        .rearrange("p (t h s) -> p t h s", t=2, h=KC) for i in (1, 2))
        logits = sb("logits", [P, B * C, E])
        biased = sb("biased", [P, B * C, E])
        rank_a, rank_b = (t[:].rearrange("p a s -> p (a s)").rearrange("p (t n) -> p t n", t=B * C)
                          for t in (d_sb, p_sb))
        rank = sb("rank", [P, B * C, E])
        probs = sb("probs", [P, B * C, E])
        total = sb("total", [P, B * C])
        weight = sb("weight", [P, B * C, NE])

        bank = [es.enter_context(nc.psum_tensor(f"bank{i}", [P, 512], F32)) for i in range(8)]

        l_x = [sem(f"l_x{b}") for b in range(B)]
        l_kT = [sem(f"l_kT{b}") for b in range(B)]
        l_ctx = [sem(f"l_ctx{b}") for b in range(B)]
        l_w = [sem(f"l_w{i}") for i in range(3)]
        l_gate, l_bias, l_consts, l_route = sem("l_gate"), sem("l_bias"), sem("l_consts"), sem("l_route")
        stored = sem("stored")
        g_step = sem("g_step")
        ident_ok, ident_b_ok, const_ok, ones_ok = sem("ident_ok"), sem("ident_b_ok"), sem("const_ok"), sem("ones_ok")
        before_ok = sem("before_ok")
        tanh_ok, gain_ok = sem("tanh_ok"), sem("gain_ok")
        pad_ok = sem("pad_ok")
        v_step = sem("v_step")
        mv1_ok, var1_ok, rs1_ok, q_ok, qT_psum = (sem(n) for n in ("mv1_ok", "var1_ok", "rs1_ok", "q_ok", "qT_psum"))
        gates_ok, f_abs_ok, f_exp_ok, f_log_ok, a_ok, r1_ok, mid_ok, am3_ok = (
            sem(n) for n in ("gates_ok", "f_abs_ok", "f_exp_ok", "f_log_ok", "a_ok", "r1_ok", "mid_ok", "am3_ok"))
        m_ok, state_row_ok, rows_ok, rows_psum, ex_ok = (sem(n) for n in ("m_ok", "state_row_ok", "rows_ok", "rows_psum", "ex_ok"))
        decay_row_ok, decay_exp_ok, decay_psum, decay_ok = (sem(n) for n in ("decay_row_ok", "decay_exp_ok", "decay_psum", "decay_ok"))
        ones_v_ok, zero_ok, sel_ok = sem("ones_v_ok"), sem("zero_ok"), sem("sel_ok")
        k_hi_ok, k_lo_ok, q_hi_ok, q_lo_ok, neg1_ok, decay_wide_ok, gate_lo_ok, head_rows_ok = (
            sem(n) for n in ("k_hi_ok", "k_lo_ok", "q_hi_ok", "q_lo_ok", "neg1_ok", "decay_wide_ok", "gate_lo_ok", "head_rows_ok"))
        l_pad = [sem(f"l_pad{h}") for h in range(HG)]
        state_hi_ok, state_lo_ok, negA_ok, negB_ok = (
            sem(n) for n in ("state_hi_ok", "state_lo_ok", "negA_ok", "negB_ok"))
        k_wt_ok, d_ok, exp_ok, qk_ok, p_ok, pv_ok, pv_all = (
            sem(n) for n in ("k_wt_ok", "d_ok", "exp_ok", "qk_ok", "p_ok", "pv_ok", "pv_all"))
        local_ok, masked_ok, carry_ok, state_ok, inter_ok, scaled_ok, comb_ok = (
            sem(n) for n in ("local_ok", "masked_ok", "carry_ok", "state_ok", "inter_ok", "scaled_ok", "comb_ok"))
        n0_ok, n1_ok, n2_ok, n3_ok, hn_ok, stA_ok, mvA_ok, varA_ok, rsA_ok, hl_ok, gained_ok, x1_ok = (
            sem(n) for n in ("n0_ok", "n1_ok", "n2_ok", "n3_ok", "hn_ok", "stA_ok", "mvA_ok", "varA_ok", "rsA_ok", "hl_ok", "gained_ok", "x1_ok"))
        stB_ok, mvB_ok, varB_ok, rsB_ok, xn_ok = (sem(n) for n in ("stB_ok", "mvB_ok", "varB_ok", "rsB_ok", "xn_ok"))
        w_hi_ok, w_ok = sem("w_hi_ok"), sem("w_ok")
        xT_psum, xT_hi_ok, xT_f_ok, xT_lo_ok = sem("xT_psum"), sem("xT_hi_ok"), sem("xT_f_ok"), sem("xT_lo_ok")
        logit_psum, logit_ok, r_step, sel_exp_ok, weight_ok = (
            sem(n) for n in ("logit_psum", "logit_ok", "r_step", "sel_exp_ok", "weight_ok"))
        up_ok, relu_ok, hi_ok, sq_ok, lo_ok, down_ok, acc_ok = (
            sem(n) for n in ("up_ok", "relu_ok", "hi_ok", "sq_ok", "lo_ok", "down_ok", "acc_ok"))

        block = es.enter_context(nc.Block())

        @block.sync
        def _(sp):
            sp.dma_start(x_all[:, 0], x[0].rearrange("(c p) d -> p c d", p=P)).then_inc(l_x[0], 16)
            sp.dma_start(gate_raw[:], gate_w.rearrange("p j (g h) -> p j g h", g=2)).then_inc(l_gate, 16)
            sp.dma_start(gate_bias[:], gate_b).then_inc(l_bias, 16)
            sp.dma_start(consts[:], row.to_broadcast([P, D + E + 2])).then_inc(l_consts, 16)
            for b in range(1, B):
                sp.dma_start(x_all[:, b], x[b].rearrange("(c p) d -> p c d", p=P)).then_inc(l_x[b], 16)
            for b in range(B):
                sp.dma_start(kT_stage[:, b], ctxT[b].rearrange("(k p) s -> p k s", p=P)).then_inc(l_kT[b], 16)
            for b in range(B):
                for c in range(C):
                    sp.dma_start(vaug[:, b, c, :, 0:DH], ctx[b, c * P:(c + 1) * P, :].rearrange("p (h d) -> p h d", h=NH))\
                        .then_inc(l_ctx[b], 16)
            sp.dma_start(route[:], route_w).then_inc(l_route, 16)

            def pad_group(b, hg):
                for h in range(4):
                    r = h * DH
                    sp.dma_start(q_pad[r:r + DH, :, hg * 4 + h, :], qT2[r:r + DH, :, b, hg, :]).then_inc(l_pad[hg], 16)

            sp.wait_ge(zero_ok, 1)
            sp.wait_ge(q_hi_ok, KC)
            sp.wait_ge(q_lo_ok, KC)
            pad_group(0, 0)
            pad_group(0, 1)
            sp.wait_ge(q_hi_ok, KC * B)
            sp.wait_ge(q_lo_ok, KC * B)
            with sp.Fori(1, B) as b:
                for hg in range(HG):
                    sp.wait_ge(qk_ok, (b - 1) * NH + 4 * (hg + 1))
                    pad_group(b, hg)
            for b in range(B):
                sp.wait_ge(acc_ok, (NE - 1) * B + b + 1)
                sp.dma_start(out[b].rearrange("(c p) d -> p c d", p=P), x_all[:, b]).then_inc(stored, 16)
            sp.wait_ge(stored, 16 * B)

        @block.gpsimd
        def _(gp):
            g = nc.gpsimd
            g.memset(ident[:], 0.0).then_inc(g_step, 1)
            gp.wait_ge(g_step, 1)
            g.affine_select(out=ident[:], in_=ident[:], compare_op=ALU.not_equal, fill=1.0, base=0,
                            pattern=[[-1, P]], channel_multiplier=1).then_inc(ident_ok, 1)
            g.memset(eps_c[:], LN_EPS)
            g.memset(minus1[:], -1.0)
            g.memset(neg_half[:], -0.5).then_inc(g_step, 1)
            gp.wait_ge(g_step, 2)

            def rsqrt(mv, rs, nb, var_ok, neg_ok, n, done):
                g.tensor_tensor(mv[:, :, 1], mv[:, :, 1], eps_c[:], ALU.add)
                g.tensor_tensor(mv[:, :, 0], mv[:, :, 0], minus1[:], ALU.mult).then_inc(var_ok, 1)
                gp.wait_ge(var_ok, n)
                g.tensor_tensor(rs, mv[:, :, 1], neg_half[:], ALU.pow).then_inc(neg_ok, 1)
                gp.wait_ge(neg_ok, n)
                g.tensor_tensor(nb, mv[:, :, 0], rs, ALU.mult).then_inc(done, 1)

            g.memset(gate_pad[:], 0.0).then_inc(g_step, 1)
            gp.wait_ge(l_gate, 16)
            g.tensor_copy(gate_sum[:, 0:KC], gate_raw[:, 0:KC])
            g.tensor_add(gate_sum[:, KC:], gate_raw[:, KC:2 * KC], gate_raw[:, 2 * KC:]).then_inc(g_step, 1)
            gp.wait_ge(g_step, 4)
            flat = gate_sum[:].rearrange("p k g h -> p k (g h)")
            g.tensor_copy(gate_part[:, 0], flat).then_inc(g_step, 1)
            gp.wait_ge(g_step, 5)
            g.tensor_tensor(gate_part[:, 1], flat, gate_part[:, 0], ALU.subtract).then_inc(g_step, 1)
            gp.wait_ge(g_step, 6)
            for b in range(B):
                for gate in range(2):
                    at = gate * NBH + b * NH
                    last = g.tensor_copy(gate_pad[:, b, :, :, at:at + NH],
                                         gate_part[:, :, :, gate * NH:(gate + 1) * NH].rearrange("p t k h -> p k t h"))
            last.then_inc(pad_ok, 1)
            g.memset(zeros_c[:], 0.0).then_inc(g_step, 1)
            g.memset(pick3[:], 0.0).then_inc(g_step, 1)
            gp.wait_ge(g_step, 8)
            for q in range(3):
                g.affine_select(out=pick3[:], in_=pick3[:], compare_op=ALU.not_equal, fill=1.0,
                                base=-NBH * q, pattern=[[-1, NBH]], channel_multiplier=1).then_inc(g_step, 1)
                gp.wait_ge(g_step, 9 + q)

            def k_low(b):
                gp.wait_ge(k_hi_ok, b + 1)
                g.tensor_tensor(kT2[:, 1, b].rearrange("p k s -> p (k s)"), kT_stage[:, b].rearrange("p k s -> p (k s)"),
                                kT2[:, 0, b].rearrange("p k s -> p (k s)"), ALU.subtract).then_inc(k_lo_ok, 1)

            for b in range(B):
                gp.wait_ge(mv1_ok, b + 1)
                rsqrt(mv1[:, b % 2], rs1[:, b % 2], nb1[:, b % 2], var1_ok, neg1_ok, b + 1, rs1_ok)
                if b == 0:
                    g.memset(q_pad[:].rearrange("p t h s -> p (t h s)").bitcast(F32), 0.0).then_inc(zero_ok, 1)
                else:
                    k_low(b - 1)
            k_low(B - 1)
            g.memset(ones_row[:], 1.0).then_inc(ones_ok, 1)
            g.affine_select(out=mask[:], in_=zeros_c[:].rearrange("p (c s) -> p c s", c=C),
                            compare_op=ALU.is_ge, fill=NEG, base=0,
                            pattern=[[0, C], [1, P]], channel_multiplier=-1).then_inc(const_ok, 1)
            g.tensor_copy(ident_b[:], ident[:]).then_inc(const_ok, 1)
            g.memset(block_mask[:], SCALE).then_inc(g_step, 1)
            gp.wait_ge(g_step, 12)
            blocks = block_mask[:].rearrange("p (h d) -> p h d", h=4)
            g.affine_select(out=blocks, in_=blocks, compare_op=ALU.is_ge, fill=0.0, base=0,
                            pattern=[[-DH, 4], [0, DV]], channel_multiplier=1).then_inc(g_step, 1)
            gp.wait_ge(g_step, 13)
            g.affine_select(out=blocks, in_=blocks, compare_op=ALU.is_ge, fill=0.0, base=DH - 1,
                            pattern=[[DH, 4], [0, DV]], channel_multiplier=-1).then_inc(const_ok, 1)
            g.memset(vaug[:, :, :, :, DH:DV].rearrange("p b c h o -> p (b c h) o"), 1.0).then_inc(ones_v_ok, 1)
            gp.wait_ge(m_ok, 1)
            g.tensor_tensor(rows[0:32].rearrange("p (c s) -> p c s", c=C),
                            am[:, 0].rearrange("p (c s) -> p c s", c=C),
                            am[:, 1].rearrange("p (c s) -> p c s", c=C)[:, :, P - 1:P].to_broadcast([NBH, C, P]),
                            ALU.add).then_inc(state_row_ok, 1)

            def weigh_keys(b):
                if not isinstance(b, int) or b > 0:
                    gp.wait_ge(local_ok, b * HG)
                g.tensor_tensor(k_wt[:].rearrange("p c (h d) -> p c h d", h=NH),
                                vaug[:, b, 0:C - 1, :, 0:DH],
                                ex[:, 0:C - 1, bass.ds(b * NH, NH)].unsqueeze(3).to_broadcast([P, C - 1, NH, DH]),
                                ALU.mult).then_inc(k_wt_ok, 1)

            def attention_norm(t):
                gp.wait_ge(mvA_ok, t + 1)
                rsqrt(mv2, rs2[:], nb2[:], varA_ok, negA_ok, t + 1, rsA_ok)

            def add_residual(t):
                gp.wait_ge(hl_ok, t + 1)
                g.tensor_tensor(h_n[:], h_n[:], ln_gain[:].unsqueeze(1).to_broadcast([P, C, D]),
                                ALU.mult).then_inc(gained_ok, 1)
                gp.wait_ge(gained_ok, t + 1)
                g.tensor_tensor(x_all[:, t].rearrange("p c d -> p (c d)"),
                                x_all[:, t].rearrange("p c d -> p (c d)"),
                                h_n[:].rearrange("p c d -> p (c d)"), ALU.add).then_inc(x1_ok, 1)

            def expert_norm(t):
                gp.wait_ge(mvB_ok, t + 1)
                rsqrt(mv2, rs2[:], nb2[:], varB_ok, negB_ok, t + 1, rsB_ok)

            def low_part(b, i):
                e = 3 * (b - 1) + i
                gp.wait_ge(w_hi_ok, e + 1)
                g.tensor_tensor(w_lo[:, e].rearrange("p a k d -> p (a k d)"),
                                w_stage[:, i].rearrange("p a k d -> p (a k d)"),
                                w_hi[:, e].rearrange("p a k d -> p (a k d)"), ALU.subtract).then_inc(w_ok, 1)

            gp.wait_ge(ex_ok, 1)
            gp.wait_ge(l_ctx[0], 16 * C)
            weigh_keys(0)
            g.memset(before[:], 1.0).then_inc(g_step, 1)
            gp.wait_ge(g_step, 14)
            g.affine_select(out=before[:], in_=before[:], compare_op=ALU.is_gt, fill=0.0, base=0,
                            pattern=[[1, E], [-1, E]], channel_multiplier=0).then_inc(before_ok, 1)
            g.memset(total[:], 0.0).then_inc(w_ok, 1)
            gp.wait_ge(gain_ok, 1)
            gp.wait_ge(am3_ok, 1)
            gp.wait_ge(mid_ok, 1)
            for b in range(1, B):
                gp.wait_ge(l_ctx[b], 16 * C)
            with gp.Fori(1, B) as b:
                weigh_keys(b)
                attention_norm(b - 1)
                low_part(b, 0)
                add_residual(b - 1)
                low_part(b, 1)
                expert_norm(b - 1)
                low_part(b, 2)
            attention_norm(B - 1)
            add_residual(B - 1)
            expert_norm(B - 1)

        @block.tensor
        def _(pe):
            mm = nc.tensor.matmul

            def transpose_q(b):
                if b >= 2:
                    pe.wait_ge(q_lo_ok, KC * (b - 1))
                pe.wait_ge(q_ok, b + 1)
                for k in range(KC):
                    for c in range(C):
                        last = nc.tensor.transpose(bank[2 + 2 * (b % 2) + k][:, c * P:(c + 1) * P],
                                                   q_tok[:, b % 2, c, k * P:(k + 1) * P], ident[:])
                    last.then_inc(qT_psum, 1)

            def gates(b, half, data):
                for k in range(KC):
                    for part in range(2):
                        last = mm(bank[0][:], gate_pad[:, b, half + k].rearrange("p t m -> p (t m)"), data[:, part, b, k, :],
                                  start=(b == 0 and half == KC and k + part == 0),
                                  stop=(b == B - 1 and half == 0 and k + part == KC))
                return last

            def gates_q(b):
                pe.wait_ge(q_lo_ok, KC * (b + 1))
                return gates(b, 0, qT2)

            def gates_ctx(b):
                pe.wait_ge(k_lo_ok, b + 1)
                gates(b, KC, kT2)

            pe.wait_ge(ident_ok, 1)
            transpose_q(0)
            pe.wait_ge(pad_ok, 1)
            for b in range(B):
                if b + 1 < B:
                    transpose_q(b + 1)
                gates_ctx(b)
                last = gates_q(b)
            last.then_inc(gates_ok, 1)

            def head_scores(b, j):
                n = b * NH + j
                free = not isinstance(b, int) or n >= 2
                if free:
                    pe.wait_ge(exp_ok, n - 1)
                pick = pick3[:, bass.ds(n, 1)].to_broadcast([96, P])
                mm(bank[j % 2][:], pick, am3[:, 1, :], start=True, stop=False)
                for c in range(C):
                    mm(bank[j % 2][:, c * P:(c + 1) * P], am3[:, 0, c * P:(c + 1) * P], pick,
                       start=False, stop=False)
                mm(bank[j % 2][:], ident_b[:], mask[:].rearrange("p c s -> p (c s)"),
                   start=False, stop=True).then_inc(d_ok, 1)
                if j % 4 == 0:
                    pe.wait_ge(l_pad[j // 4], 64 * (b + 1))
                if free:
                    pe.wait_ge(p_ok, n - 1)
                for c in range(C):
                    at = slice(c * P, (c + 1) * P)
                    for m, (kp, qp) in enumerate(((0, 0), (0, 1), (1, 0))):
                        last = mm(bank[2 + j % 2][:, at], kT2[:, kp, b, j // 4, at], q_pad[:, qp, j, at],
                                  start=(m == 0), stop=(m == MIXED - 1))
                last.then_inc(qk_ok, 1)

            def head_values(b, j):
                n = b * NH + j
                pe.wait_ge(p_ok, n + 1)
                if j % 4 == 0 and (not isinstance(b, int) or n > 0):
                    pe.wait_ge(comb_ok, b * HG + j // 4)
                for c in range(C):
                    at = (c % 2) * GV + (j % 4) * DV
                    last = mm(bank[4 + c // 2][:, at:at + DV], p_sb[:, j % 2, c * P:(c + 1) * P],
                              vaug[:, b, c, j, :], start=True, stop=True)
                last.then_inc(pv_ok, 1)

            def group_state(b, hg):
                if hg == 0:
                    pe.wait_ge(k_wt_ok, b + 1)
                if not isinstance(b, int) or b + hg > 0:
                    pe.wait_ge(masked_ok, b * HG + hg)
                for c in range(C - 1):
                    last = mm(bank[7][:, c * GV:(c + 1) * GV], k_wt[:, c, hg * P:(hg + 1) * P],
                              vaug[:, b, c, hg * 4:hg * 4 + 4, :].rearrange("p h d -> p (h d)"), start=True, stop=True)
                last.then_inc(local_ok, 1)

            def group_inter(b, hg):
                pe.wait_ge(state_lo_ok, b * HG + hg + 1)
                if not isinstance(b, int) or b + hg > 0:
                    pe.wait_ge(comb_ok, b * HG + hg)
                for c in range(1, C):
                    for m, (qp, part) in enumerate(((0, 0), (0, 1), (1, 0))):
                        last = mm(bank[6][:, (c - 1) * GV:c * GV], qT2[:, qp, b, hg, c * P:(c + 1) * P],
                                  state2[:, part, hg, c - 1, :], start=(m == 0), stop=(m == MIXED - 1))
                last.then_inc(inter_ok, 1)

            def batch(b):
                for j in range(NH):
                    head_scores(b, j)
                    if j % 4 == 0:
                        group_state(b, j // 4)
                    if j > 0:
                        head_values(b, j - 1)
                    if j % 4 == 3:
                        group_inter(b, j // 4)
                head_values(b, NH - 1)

            pe.wait_ge(rows_ok, 1)
            pe.wait_ge(state_row_ok, 1)
            for c in range(C):
                last = nc.tensor.transpose(bank[1][:, c * 96:(c + 1) * 96], rows[:, c * P:(c + 1) * P],
                                           ident[0:96, 0:96])
            last.then_inc(rows_psum, 1)
            pe.wait_ge(decay_wide_ok, 1)
            pe.wait_ge(head_rows_ok, 1)
            mm(bank[7][:, 0:4 * B], head_rows[:],
               decay_wide[:].rearrange("r n t -> r (n t)"), start=True, stop=True).then_inc(decay_psum, 1)
            pe.wait_ge(const_ok, 3)
            pe.wait_ge(am3_ok, 1)
            pe.wait_ge(mid_ok, 1)
            pe.wait_ge(ex_ok, 1)
            pe.wait_ge(decay_ok, 1)
            pe.wait_ge(a_ok, 1)
            pe.wait_ge(ones_v_ok, 1)
            pe.wait_ge(l_ctx[0], 16 * C)
            batch(0)
            for b in range(1, B):
                pe.wait_ge(l_ctx[b], 16 * C)
            with pe.Fori(1, B) as b:
                batch(b)

            def transpose_x(b, lo):
                pe.wait_ge(xn_ok, b + 1)
                for k in range(KC):
                    for c in range(C):
                        last = nc.tensor.transpose(bank[lo + k][:, c * P:(c + 1) * P],
                                                   xn[:, b, c, k * P:(k + 1) * P], ident[:])
                    last.then_inc(xT_psum, 1)

            def router(b, to, at):
                pe.wait_ge(xT_f_ok, KC * (b + 1))
                for c in range(C):
                    for k in range(KC):
                        last = mm(to[:, at + c * E:at + (c + 1) * E], xT[:, b, k, c * P:(c + 1) * P], route[:, k, :],
                                  start=(k == 0), stop=(k == KC - 1))
                last.then_inc(logit_psum, 1)

            def up(e, b):
                n = e * B + b
                if b == 0:
                    pe.wait_ge(w_ok, e + 2)
                if not isinstance(n, int) or n >= 2:
                    pe.wait_ge(relu_ok, KC * (n - 1))
                for h in range(KC):
                    for k in range(KC):
                        for m, (w, xx) in enumerate(((w_hi, xT_hi), (w_hi, xT_lo), (w_lo, xT_hi))):
                            last = mm(bank[2 * (b % 2) + h][:], w[:, e, 0, k, h * P:(h + 1) * P], xx[:, b, k, :],
                                      start=(k == 0 and m == 0), stop=(k == KC - 1 and m == MIXED - 1))
                    last.then_inc(up_ok, 1)

            def down(e, b):
                n = e * B + b
                pe.wait_ge(hi_ok, KC * (n + 1))
                pe.wait_ge(lo_ok, KC * (n + 1))
                if not isinstance(n, int) or n >= 2:
                    pe.wait_ge(acc_ok, n - 1)
                for c in range(C):
                    for h in range(KC):
                        for m, (s, w) in enumerate(((sq_hi, w_hi), (sq_hi, w_lo), (sq_lo, w_hi))):
                            at = (c % 2) * D
                            last = mm(bank[4 + 2 * (b % 2) + c // 2][:, at:at + D],
                                      s[:, b % 2, h, c * P:(c + 1) * P], w[:, e, 1, h, :],
                                      start=(h == 0 and m == 0), stop=(h == KC - 1 and m == MIXED - 1))
                last.then_inc(down_ok, 1)

            pe.wait_ge(comb_ok, HG * B)
            pe.wait_ge(l_route, 16)
            transpose_x(0, 4)
            transpose_x(1, 6)
            transpose_x(2, 0)
            pe.wait_ge(xT_lo_ok, KC * 3)
            pe.wait_ge(xT_f_ok, KC * 3)
            pe.wait_ge(xT_hi_ok, KC * 3)
            for b in range(3):
                router(b, bank[2], b * C * E)
            up(0, 0)
            pe.wait_ge(logit_ok, 1)
            up(0, 1)
            down(0, 0)
            transpose_x(3, 6)
            pe.wait_ge(xT_lo_ok, KC * 4)
            pe.wait_ge(xT_hi_ok, KC * 4)
            router(3, bank[6], 0)
            up(0, 2)
            pe.wait_ge(logit_ok, 2)
            down(0, 1)
            up(0, 3)
            down(0, 2)
            with pe.Fori(1, NE) as e:
                up(e, 0)
                down(e - 1, B - 1)
                for b in range(1, B):
                    up(e, b)
                    down(e, b - 1)
            down(NE - 1, B - 1)

        @block.scalar
        def _(act):
            s = nc.scalar
            act.wait_ge(l_consts, 16)
            s.activation(tanhs[:], consts[:, D + E:D + E + 2], ACT.Tanh).then_inc(tanh_ok, 1)
            s.preload_act_table_set("natural_log_exp_and_others")

            def normalise(to, data, rs, nb, done):
                for c in range(C):
                    last = s.activation(to[:, c, :], data[:, c, :], ACT.Identity, bias=nb[:, c:c + 1], scale=rs[:, c:c + 1])
                last.then_inc(done, 1)

            def normalise_x(b):
                act.wait_ge(rs1_ok, b + 1)
                if b >= 2:
                    act.wait_ge(qT_psum, KC * (b - 1))
                normalise(q_tok[:, b % 2], x_all[:, b], rs1[:, b % 2], nb1[:, b % 2], q_ok)

            normalise_x(0)
            for b in range(B):
                if b + 1 < B:
                    normalise_x(b + 1)
                act.wait_ge(l_kT[b], 16)
                s.activation(kT2[:, 0, b].rearrange("p k s -> p (k s)"), kT_stage[:, b].rearrange("p k s -> p (k s)"),
                             ACT.Copy).then_inc(k_hi_ok, 1)
                for k in range(KC):
                    act.wait_ge(qT_psum, KC * b + k + 1)
                    s.activation(qT2[:, 0, b, k, :], bank[2 + 2 * (b % 2) + k][:], ACT.Copy).then_inc(q_hi_ok, 1)
            act.wait_ge(gates_ok, 1)
            for gate in (1, 0):
                at = 2 * NBH + gate * NBH
                s.activation(lo_rows[:, gate], bank[0][at:at + NBH, :], ACT.Copy).then_inc(gate_lo_ok, 1)
            act.wait_ge(f_abs_ok, 1)
            s.activation(f_abs, f_abs, ACT.Exp, scale=-1.0).then_inc(f_exp_ok, 1)
            act.wait_ge(f_exp_ok, 1)
            s.activation(f_abs, f_abs, ACT.Ln, bias=1.0).then_inc(f_log_ok, 1)
            act.wait_ge(r1_ok, 1)
            s.activation(am3[32:64], am_rest, ACT.Copy).then_inc(mid_ok, 1)
            act.wait_ge(decay_row_ok, 1)
            s.activation(decay_exp[:], decay_row[:], ACT.Exp).then_inc(decay_exp_ok, 1)
            act.wait_ge(rows_psum, 1)
            s.activation(ex[:].rearrange("p c r -> p (c r)"), bank[1][:, 0:C * 96], ACT.Exp).then_inc(ex_ok, 1)
            act.wait_ge(decay_psum, 1)
            s.activation(decay[:].rearrange("p n t -> p (n t)"), bank[7][:, 0:4 * B], ACT.Copy).then_inc(decay_ok, 1)

            def head_exp(b, j):
                n = b * NH + j
                act.wait_ge(d_ok, n + 1)
                if not isinstance(b, int) or n >= 2:
                    act.wait_ge(p_ok, n - 1)
                s.activation(d_sb[:, j % 2, :], bank[j % 2][:], ACT.Exp).then_inc(exp_ok, 1)

            def high_part(b, i):
                e = 3 * (b - 1) + i
                act.wait_ge(l_w[i], 16 * b)
                s.activation(w_hi[:, e].rearrange("p a k d -> p (a k d)"),
                             w_stage[:, i].rearrange("p a k d -> p (a k d)"), ACT.Copy).then_inc(w_hi_ok, 1)

            def state_high(b, hg):
                n = b * HG + hg
                act.wait_ge(state_ok, n + 1)
                if not isinstance(b, int) or b > 0:
                    act.wait_ge(inter_ok, n - 1)
                s.activation(state2[:, 0, hg], state[:, hg], ACT.Copy).then_inc(state_hi_ok, 1)

            def load_experts(b):
                act.wait_ge(w_ok, 3 * (b - 1) + 1)
                for i in range(3):
                    act.dma_start(w_stage[:, i], experts[:, 3 * (b - 1) + i]).then_inc(l_w[i], 16)

            def normaliseA(t):
                act.wait_ge(rsA_ok, t + 1)
                normalise(h_n[:], h_n[:], rs2[:], nb2[:], hl_ok)

            def normaliseB(t):
                act.wait_ge(rsB_ok, t + 1)
                normalise(xn[:, t], x_all[:, t], rs2[:], nb2[:], xn_ok)

            for j in range(NH):
                head_exp(0, j)
                if j % 4 == 1:
                    state_high(0, j // 4)
            with act.Fori(1, B) as b:
                load_experts(b)
                for j in range(NH):
                    head_exp(b, j)
                    if j % 4 == 1:
                        state_high(b, j // 4)
                    if j in (3, 4, 6):
                        high_part(b, (3, 4, 6).index(j))
                    if j == 5:
                        normaliseA(b - 1)
                normaliseB(b - 1)

            def copy_x(b, lo):
                for k in range(KC):
                    act.wait_ge(xT_psum, KC * b + k + 1)
                    s.activation(xT_hi[:, b, k, :], bank[lo + k][:], ACT.Copy).then_inc(xT_hi_ok, 1)
                    s.activation(xT[:, b, k, :], bank[lo + k][:], ACT.Copy).then_inc(xT_f_ok, 1)

            def relu(e, b):
                n = e * B + b
                for h in range(KC):
                    act.wait_ge(up_ok, KC * n + h + 1)
                    if not isinstance(n, int) or n >= 2:
                        act.wait_ge(sq_ok, KC * (n - 2) + h + 1)
                    s.activation(relu_z[:, b % 2, h, :], bank[2 * (b % 2) + h][:], ACT.Relu).then_inc(relu_ok, 1)
                for h in range(KC):
                    act.wait_ge(relu_ok, KC * n + h + 1)
                    if not isinstance(n, int) or n >= 2:
                        act.wait_ge(down_ok, n - 1)
                    s.activation(sq_hi[:, b % 2, h, :], relu_z[:, b % 2, h, :], ACT.Square).then_inc(hi_ok, 1)

            copy_x(0, 4)
            copy_x(1, 6)
            copy_x(2, 0)
            normaliseA(B - 1)
            act.wait_ge(logit_psum, 3)
            s.activation(logits[:, 0:3 * C].rearrange("p t e -> p (t e)"), bank[2][:, 0:3 * C * E],
                         ACT.Copy).then_inc(logit_ok, 1)
            relu(0, 0)
            normaliseB(B - 1)
            relu(0, 1)
            copy_x(3, 6)
            act.wait_ge(logit_psum, 4)
            s.activation(logits[:, 3 * C:].rearrange("p t e -> p (t e)"), bank[6][:, 0:C * E],
                         ACT.Copy).then_inc(logit_ok, 1)
            act.wait_ge(logit_ok, 2)
            s.activation(probs[:], logits[:], ACT.Exp, scale=-1.0).then_inc(sel_exp_ok, 1)
            relu(0, 2)
            relu(0, 3)
            with act.Fori(1, NE) as e:
                for b in range(B):
                    relu(e, b)

        @block.vector
        def _(dve):
            v = nc.vector
            steps = [0]

            def step(ins):
                steps[0] += 1
                ins.then_inc(v_step, 1)
                dve.wait_ge(v_step, steps[0])

            def stats(b):
                dve.wait_ge(l_x[b], 16)
                if b >= 2:
                    dve.wait_ge(rs1_ok, b - 1)
                for c in range(C):
                    last = v.bn_stats(st1[:, b % 2, c, :], x_all[:, b, c, :])
                step(last)
                for c in range(C):
                    last = v.bn_aggr(mv1[:, b % 2, c, :], st1[:, b % 2, c, :])
                last.then_inc(mv1_ok, 1)

            def low_q(b):
                for k in range(KC):
                    dve.wait_ge(q_hi_ok, KC * b + k + 1)
                    v.tensor_tensor(qT2[:, 1, b, k, :], bank[2 + 2 * (b % 2) + k][:], qT2[:, 0, b, k, :],
                                    ALU.subtract).then_inc(q_lo_ok, 1)

            dve.wait_ge(ident_ok, 1)
            v.tensor_reduce(is_head[:], ident[0:NBH, 0:NBH].rearrange("p (n h) -> p h n", h=4), AX.X, ALU.add)
            v.tensor_reduce(is_group[:], ident[0:NBH, 0:NBH].rearrange("p (n h) -> p n h", h=4), AX.X,
                            ALU.add).then_inc(sel_ok, 1)
            dve.wait_ge(sel_ok, 1)
            v.tensor_copy(head_rows[:].rearrange("r (h d) -> r h d", h=4),
                          is_head[:].unsqueeze(2).to_broadcast([NBH, 4, DH])).then_inc(head_rows_ok, 1)
            step(v.memset(rows[32:64, 0:P], 0.0))
            stats(0)
            stats(1)
            for b in range(B):
                if b + 2 < B:
                    stats(b + 2)
                low_q(b)
            dve.wait_ge(tanh_ok, 1)
            v.tensor_scalar(ln_gain[:], consts[:, 0:D], tanhs[:, 0:1], None, ALU.mult).then_inc(gain_ok, 1)

            dve.wait_ge(gates_ok, 1)
            dve.wait_ge(l_bias, 16)
            dve.wait_ge(gate_lo_ok, 1)
            step(v.scalar_tensor_tensor(f_pre, bank[0][NBH:2 * NBH, :], gate_bias[:, 1:2], lo_rows[:, 1],
                                        ALU.add, ALU.add))
            v.scalar_tensor_tensor(f_abs, f_pre, -1.0, f_pre, ALU.mult, ALU.max).then_inc(f_abs_ok, 1)
            dve.wait_ge(gate_lo_ok, 2)
            step(v.scalar_tensor_tensor(am[:, 0], bank[0][0:NBH, :], gate_bias[:, 0:1], lo_rows[:, 0],
                                        ALU.add, ALU.add))
            dve.wait_ge(f_log_ok, 1)
            step(v.scalar_tensor_tensor(log_f, f_pre, 0.0, f_abs, ALU.min, ALU.subtract))
            dve.wait_ge(ones_ok, 1)
            step(v.tensor_tensor_scan(cs, log_f, ones_row[:], 0.0, ALU.add, ALU.mult))
            dve.wait_ge(sel_ok, 1)
            v.tensor_tensor(am[:, 0], am[:, 0], cs, ALU.subtract).then_inc(a_ok, 1)
            dve.wait_ge(a_ok, 1)
            step(v.tensor_tensor_scan(f_pre, am[:, 0], am[:, 0], LOWEST, ALU.max, ALU.max))
            step(v.tensor_scalar(am[:, 1], f_pre, -1.0, None, ALU.mult))
            m_row = f_pre
            m_end = f_pre.rearrange("p (c s) -> p c s", c=C)[:, :, P - 1:P]
            v.tensor_copy(am3[0:32], am).then_inc(m_ok, 1)
            v.tensor_tensor(decay_row[:].unsqueeze(2), m_end[:, 0:2], m_end[:, 1:3], ALU.subtract)\
                .then_inc(decay_row_ok, 1)
            dve.wait_ge(m_ok, 1)
            v.tensor_tensor(am_rest, am, am3[0:32], ALU.subtract).then_inc(r1_ok, 1)
            v.tensor_tensor(rows[32:64, P:].rearrange("p (c s) -> p c s", c=C - 1),
                            m_end[:, 0:C - 1].to_broadcast([NBH, C - 1, P]),
                            m_row[:, P:].rearrange("p (c s) -> p c s", c=C - 1), ALU.subtract)
            v.scalar_tensor_tensor(rows[64:96], cs, -1.0, m_row[:], ALU.mult, ALU.subtract).then_inc(rows_ok, 1)
            dve.wait_ge(r1_ok, 1)
            step(v.tensor_copy(am_mid, am_rest))
            v.tensor_tensor(am3[64:96], am_rest, am_mid, ALU.subtract).then_inc(am3_ok, 1)
            dve.wait_ge(decay_exp_ok, 1)
            v.tensor_tensor(decay_wide[:], decay_exp[:].unsqueeze(1).to_broadcast([NBH, B * HG, 2]),
                            is_group[:].unsqueeze(2).to_broadcast([NBH, B * HG, 2]), ALU.mult).then_inc(decay_wide_ok, 1)

            def head_product(b, j):
                n = b * NH + j
                dve.wait_ge(exp_ok, n + 1)
                dve.wait_ge(qk_ok, n + 1)
                if not isinstance(b, int) or n >= 2:
                    dve.wait_ge(pv_ok, n - 1)
                v.scalar_tensor_tensor(p_sb[:, j % 2, :], bank[2 + j % 2][:], SCALE, d_sb[:, j % 2, :],
                                       ALU.mult, ALU.mult).then_inc(p_ok, 1)

            def group_states(b, hg):
                n = b * HG + hg
                dve.wait_ge(local_ok, n + 1)
                if not isinstance(b, int) or b > 0:
                    dve.wait_ge(state_lo_ok, n - 1)
                v.tensor_tensor(state[:, hg], bank[7][:, 0:(C - 1) * GV].rearrange("p (c g) -> p c g", c=C - 1),
                                block_mask[:].unsqueeze(1).to_broadcast([P, C - 1, GV]), ALU.mult).then_inc(masked_ok, 1)
                dve.wait_ge(masked_ok, n + 1)
                v.scalar_tensor_tensor(state[:, hg, 1], state[:, hg, 0], decay[:, n, 0:1], state[:, hg, 1],
                                       ALU.mult, ALU.add).then_inc(carry_ok, 1)
                dve.wait_ge(carry_ok, n + 1)
                v.scalar_tensor_tensor(state[:, hg, 2], state[:, hg, 1], decay[:, n, 1:2], state[:, hg, 2],
                                       ALU.mult, ALU.add).then_inc(state_ok, 1)

            def state_low(b, hg):
                n = b * HG + hg
                dve.wait_ge(state_hi_ok, n + 1)
                v.tensor_tensor(state2[:, 1, hg], state[:, hg], state2[:, 0, hg], ALU.subtract).then_inc(state_lo_ok, 1)

            def group_combine(b, hg):
                n = b * HG + hg
                dve.wait_ge(inter_ok, n + 1)
                v.tensor_tensor(carried[:].rearrange("p c (h d) -> p c h d", h=4),
                                bank[6][:, 0:(C - 1) * GV].rearrange("p (c h d) -> p c h d", c=C - 1, h=4),
                                ex[:, 1:C, bass.ds(NBH + n * 4, 4)].unsqueeze(3).to_broadcast([P, C - 1, 4, DV]),
                                ALU.mult).then_inc(scaled_ok, 1)
                dve.wait_ge(pv_ok, (n + 1) * 4)
                h4 = h_sum[:, :, hg * 4:hg * 4 + 4, :].rearrange("p c h d -> p c (h d)")
                v.tensor_copy(h4[:, 0], bank[4][:, 0:GV])
                dve.wait_ge(scaled_ok, n + 1)
                v.tensor_tensor(h4[:, 1], bank[4][:, GV:2 * GV], carried[:, 0], ALU.add)
                v.tensor_tensor(h4[:, 2:4], bank[5][:, 0:2 * GV].rearrange("p (c g) -> p c g", c=2),
                                carried[:, 1:3], ALU.add).then_inc(comb_ok, 1)

            def norm_max(t):
                dve.wait_ge(comb_ok, HG * (t + 1))
                v.scalar_tensor_tensor(norm[:, 0], h_sum[:, :, :, DH], -1.0, ex[:, :, bass.ds(2 * NBH + t * NH, NH)],
                                       ALU.mult, ALU.max).then_inc(n0_ok, 1)

            def norm_eps(t):
                dve.wait_ge(n0_ok, t + 1)
                v.tensor_tensor(norm[:, 2], norm[:, 0], h_sum[:, :, :, DH], ALU.max).then_inc(n1_ok, 1)
                dve.wait_ge(n1_ok, t + 1)
                v.tensor_scalar(norm[:, 1], norm[:, 2], EPS, None, ALU.add).then_inc(n2_ok, 1)

            def norm_divide(t):
                dve.wait_ge(n2_ok, t + 1)
                v.reciprocal(norm[:, 2], norm[:, 1]).then_inc(n3_ok, 1)
                dve.wait_ge(n3_ok, t + 1)
                v.tensor_tensor(h_n[:].rearrange("p c (h d) -> p (c h) d", h=NH),
                                h_sum[:, :, :, 0:DH].rearrange("p c h d -> p (c h) d"),
                                norm[:, 2].rearrange("p c h -> p (c h)").unsqueeze(2).to_broadcast([P, C * NH, DH]),
                                ALU.mult).then_inc(hn_ok, 1)

            def statsA(t):
                dve.wait_ge(hn_ok, t + 1)
                for c in range(C):
                    last = v.bn_stats(st2[:, c, :], h_n[:, c, :])
                last.then_inc(stA_ok, 1)

            def meanA(t):
                for c in range(C):
                    last = v.bn_aggr(mv2[:, c, :], st2[:, c, :])
                last.then_inc(mvA_ok, 1)

            def statsB(t):
                dve.wait_ge(x1_ok, t + 1)
                for c in range(C):
                    last = v.bn_stats(st2[:, c, :], x_all[:, t, c, :])
                last.then_inc(stB_ok, 1)

            def meanB(t):
                for c in range(C):
                    last = v.bn_aggr(mv2[:, c, :], st2[:, c, :])
                last.then_inc(mvB_ok, 1)

            after_head = {0: norm_max, 1: norm_eps, 2: norm_divide, 3: statsA, 4: meanA}

            def batch(b, tail):
                for j in range(NH):
                    if tail and j == 4:
                        dve.wait_ge(stA_ok, b)
                    head_product(b, j)
                    if j % 4 == 0:
                        group_states(b, j // 4)
                    if j % 4 == 2:
                        state_low(b, j // 4)
                    if tail and j in after_head:
                        after_head[j](b - 1)
                    if j == 5:
                        group_combine(b, 0)
                if tail:
                    statsB(b - 1)
                    dve.wait_ge(stB_ok, b)
                group_combine(b, 1)
                if tail:
                    meanB(b - 1)

            dve.wait_ge(decay_ok, 1)
            dve.wait_ge(const_ok, 3)
            dve.wait_ge(ex_ok, 1)
            batch(0, False)
            with dve.Fori(1, B) as b:
                batch(b, True)

            def low_x(b, lo):
                for k in range(KC):
                    dve.wait_ge(xT_f_ok, KC * b + k + 1)
                    v.tensor_tensor(xT_lo[:, b, k, :], bank[lo + k][:], xT_hi[:, b, k, :],
                                    ALU.subtract).then_inc(xT_lo_ok, 1)

            def square(e, b):
                n = e * B + b
                for h in range(KC):
                    dve.wait_ge(relu_ok, KC * n + h + 1)
                    if not isinstance(n, int) or n >= 1:
                        dve.wait_ge(lo_ok, KC * (n - 1) + h + 1)
                    v.tensor_tensor(sq[:, h, :], relu_z[:, b % 2, h, :], relu_z[:, b % 2, h, :],
                                    ALU.mult).then_inc(sq_ok, 1)
                for h in range(KC):
                    dve.wait_ge(sq_ok, KC * n + h + 1)
                    dve.wait_ge(hi_ok, KC * n + h + 1)
                    v.tensor_tensor(sq_lo[:, b % 2, h, :], sq[:, h, :], sq_hi[:, b % 2, h, :],
                                    ALU.subtract).then_inc(lo_ok, 1)

            def accumulate(e, b):
                n = e * B + b
                dve.wait_ge(down_ok, n + 1)
                if not isinstance(n, int) or n >= B:
                    dve.wait_ge(acc_ok, n - B + 1)
                for c in range(C):
                    at = (c % 2) * D
                    last = v.scalar_tensor_tensor(x_all[:, b, c, :], bank[4 + 2 * (b % 2) + c // 2][:, at:at + D],
                                                  weight[:, b * C + c, bass.ds(e, 1)], x_all[:, b, c, :],
                                                  ALU.mult, ALU.add)
                last.then_inc(acc_ok, 1)

            low_x(0, 4)
            low_x(1, 6)
            low_x(2, 0)
            norm_max(B - 1)
            norm_eps(B - 1)
            norm_divide(B - 1)
            statsA(B - 1)
            dve.wait_ge(stA_ok, B)
            meanA(B - 1)
            v.tensor_copy(weight[:, :, 0], tanhs[:, 1:2].to_broadcast([P, B * C])).then_inc(r_step, 1)
            square(0, 0)
            statsB(B - 1)
            dve.wait_ge(stB_ok, B)
            meanB(B - 1)
            dve.wait_ge(r_step, 1)
            square(0, 1)
            accumulate(0, 0)
            low_x(3, 6)
            dve.wait_ge(logit_ok, 2)
            v.tensor_tensor(biased[:], logits[:], consts[:, D:D + E].unsqueeze(1).to_broadcast([P, B * C, E]),
                            ALU.add).then_inc(r_step, 1)
            dve.wait_ge(r_step, 2)
            other = biased[:].unsqueeze(2).to_broadcast([P, B * C, E, E])
            own = biased[:].unsqueeze(3).to_broadcast([P, B * C, E, E])
            four = "p t (j i) -> p t j i"
            v.tensor_tensor(rank_a[:].rearrange(four, j=E), other, own, ALU.is_gt)
            v.tensor_tensor(rank_b[:].rearrange(four, j=E), other, own, ALU.is_equal).then_inc(r_step, 1)
            square(0, 2)
            accumulate(0, 1)
            dve.wait_ge(r_step, 3)
            dve.wait_ge(before_ok, 1)
            v.tensor_tensor(rank_b[:], rank_b[:], before[:].rearrange("p j i -> p (j i)").unsqueeze(1)
                            .to_broadcast([P, B * C, E * E]), ALU.mult).then_inc(r_step, 1)
            dve.wait_ge(r_step, 4)
            v.tensor_tensor(rank_a[:], rank_a[:], rank_b[:], ALU.add).then_inc(r_step, 1)
            dve.wait_ge(r_step, 5)
            v.tensor_reduce(rank[:], rank_a[:].rearrange(four, j=E), AX.X, ALU.add).then_inc(r_step, 1)
            dve.wait_ge(sel_exp_ok, 1)
            v.tensor_scalar(probs[:], probs[:], 1.0, None, ALU.add).then_inc(r_step, 1)
            dve.wait_ge(r_step, 7)
            v.reciprocal(probs[:], probs[:]).then_inc(r_step, 1)
            dve.wait_ge(r_step, 8)
            v.scalar_tensor_tensor(probs[:], rank[:], 1.5, probs[:], ALU.is_lt, ALU.mult).then_inc(r_step, 1)
            square(0, 3)
            accumulate(0, 2)
            dve.wait_ge(r_step, 9)
            v.tensor_reduce(total[:], probs[:], AX.X, ALU.add).then_inc(r_step, 1)
            dve.wait_ge(r_step, 10)
            v.tensor_scalar(total[:], total[:], W_EPS, None, ALU.add).then_inc(r_step, 1)
            dve.wait_ge(r_step, 11)
            v.reciprocal(total[:], total[:]).then_inc(r_step, 1)
            dve.wait_ge(r_step, 12)
            v.tensor_scalar(total[:], total[:], tanhs[:, 1:2], None, ALU.mult).then_inc(r_step, 1)
            dve.wait_ge(r_step, 13)
            v.tensor_tensor(weight[:, :, 1:NE], probs[:], total[:].unsqueeze(2).to_broadcast([P, B * C, E]),
                            ALU.mult).then_inc(weight_ok, 1)
            dve.wait_ge(weight_ok, 1)
            with dve.Fori(1, NE) as e:
                square(e, 0)
                accumulate(e - 1, B - 1)
                for b in range(1, B):
                    square(e, b)
                    accumulate(e, b - 1)
            accumulate(NE - 1, B - 1)


def kernel(x, ctx_1024, g_xattn, g_ffn, L0_xattn_igate_w, L0_xattn_igate_b, L0_xattn_fgate_w, L0_xattn_fgate_b,
           L0_xattn_ln_scale, L0_ffn_gate_w, L0_ffn_lb_bias, L0_ffn_w1, L0_ffn_w2, L0_ffn_cfc, L0_ffn_cproj):
    import concourse.bacc as bacc
    from concourse.bass_utils import run_bass_kernel_spmd

    a = np.asarray

    def halves(w):
        return a(w).transpose(2, 0, 1).reshape(KC, P, -1, w.shape[1]).transpose(1, 2, 0, 3)

    up = np.concatenate([halves(a(L0_ffn_cfc)[None]), halves(a(L0_ffn_w1))], 1)
    down = np.concatenate([halves(a(L0_ffn_cproj)[None]), halves(a(L0_ffn_w2))], 1)
    gates = np.concatenate([a(L0_xattn_igate_w), a(L0_xattn_fgate_w)], 0)
    arrays = {
        "x": a(x),
        "ctx": a(ctx_1024),
        "ctxT": a(ctx_1024).transpose(0, 2, 1),
        "experts": np.stack([up, down], 2),
        "gate_w": gates.T.reshape(3 * KC, P, 2 * NH).transpose(1, 0, 2),
        "gate_b": np.stack([np.tile(a(L0_xattn_igate_b), B), np.tile(a(L0_xattn_fgate_b), B)], 1),
        "row": np.concatenate([a(L0_xattn_ln_scale), a(L0_ffn_lb_bias), a(g_xattn), a(g_ffn)])[None],
        "route_w": a(L0_ffn_gate_w).T.reshape(KC, P, E).transpose(1, 0, 2),
    }
    arrays = {n: np.ascontiguousarray(v) for n, v in arrays.items()}
    nc = bacc.Bacc("TRN2", target_bir_lowering=False, num_devices=1)
    args = {n: nc.dram_tensor(n, v.shape, F32, kind="ExternalInput").ap() for n, v in arrays.items()}
    out = nc.dram_tensor("out", (B, S, D), F32, kind="ExternalOutput").ap()
    gated_block(nc, out=out, **args)
    r = run_bass_kernel_spmd(nc, [arrays], core_ids=[0])
    return r.results[0]["out"]
```

```python
from contextlib import ExitStack

import numpy as np
import concourse.bass as bass
from concourse import mybir

F32 = mybir.dt.float32
BF16 = mybir.dt.bfloat16
ALU = mybir.AluOpType
ACT = mybir.ActivationFunctionType
AX = mybir.AxisListType

P = 128
B, S, D = 4, 512, 256
NH, DH = 8, 32
C = S // P
KC = D // P
NBH = B * NH
HG = NH // 4
DV = DH + 1
GV = 4 * DV
E = 8
NE = E + 1
PS = 4
LAG = 2
MIXED = 3
LN_EPS, EPS, W_EPS = 1e-5, 1e-6, 1e-6
SCALE = float(DH) ** -0.5
NEG = -1e30
LOWEST = -3.0e38


def gated_block(nc, x, ctx, ctxT, experts, gate_w, gate_b, row, route_w, out):
    es = ExitStack()
    with es:
        def sb(name, shape, dt=F32):
            return es.enter_context(nc.sbuf_tensor(name, shape, dt))

        def sem(name):
            return es.enter_context(nc.semaphore(name))

        x_all = sb("x_all", [P, B, C, D])
        qT2 = sb("qT2", [P, 2, B, KC, S], BF16)
        kT2 = sb("kT2", [P, 2, B, KC, S], BF16)
        q_pad = sb("q_pad", [P, 2, NH, S], BF16)
        xn = sb("xn", [P, B, C, D])
        vaug = sb("vaug", [P, B, C, NH, DV])
        w_hi = sb("w_hi", [P, NE, 2, KC, D], BF16)
        w_lo = sb("w_lo", [P, NE, 2, KC, D], BF16)
        w_stage = sb("w_stage", [P, 3, 2, KC, D])
        xT = qT2[:].rearrange("p t b k s -> p (t b k s)").bitcast(F32).rearrange("p (b k s) -> p b k s", b=B, k=KC)
        xT_hi, xT_lo = kT2[:, 0], kT2[:, 1]
        kT_stage = w_hi[:].rearrange("p e a k d -> p (e a k d)").bitcast(F32)[:, 0:B * KC * S]\
            .rearrange("p (b k s) -> p b k s", b=B, k=KC)
        ident = sb("ident", [P, P])
        ident_b = sb("ident_b", [P, P], BF16)
        mask = sb("mask", [P, C, P], BF16)
        pick3 = sb("pick3", [96, NBH], BF16)
        is_head = sb("is_head", [NBH, 4])
        head_rows = sb("head_rows", [NBH, P])
        is_group = sb("is_group", [NBH, B * HG])
        block_mask = sb("block_mask", [P, GV])
        neg_half = sb("neg_half", [P, C])
        eps_c = sb("eps_c", [P, C])
        ones_row = sb("ones_row", [NBH, S])
        before = sb("before", [P, E, E])
        consts = sb("consts", [P, D + E + 2])
        tanhs = sb("tanhs", [P, 2])
        ln_gain = sb("ln_gain", [P, D])
        gate_raw = sb("gate_raw", [P, 3 * KC, 2, NH])
        gate_sum = sb("gate_sum", [P, 2 * KC, 2, NH])
        gate_part = sb("gate_part", [P, 2, 2 * KC, 2 * NH], BF16)
        gate_pad = sb("gate_pad", [P, B, 2 * KC, 2, 2 * NBH], BF16)
        gate_bias = sb("gate_bias", [NBH, 2])
        route = sb("route", [P, KC, E])
        scratch = w_lo[0:NBH].rearrange("p e a k d -> p (e a k d)").bitcast(F32)
        f_pre, f_abs, log_f, cs = (scratch[:, i * S:(i + 1) * S] for i in range(4))
        am = scratch[:, 4 * S:6 * S].rearrange("p (t s) -> p t s", t=2)
        am_rest = scratch[:, 6 * S:8 * S].rearrange("p (t s) -> p t s", t=2)
        am_mid = scratch[:, 8 * S:9 * S].bitcast(BF16).rearrange("p (t s) -> p t s", t=2)
        am3 = sb("am3", [96, 2, S], BF16)
        rows = sb("rows", [96, S])
        decay_row = sb("decay_row", [NBH, 2])
        decay_exp = sb("decay_exp", [NBH, 2])
        decay_wide = sb("decay_wide", [NBH, B * HG, 2])
        decay = sb("decay", [P, B * HG, 2])
        ex = sb("ex", [P, C, 96])
        st1 = sb("st1", [P, B, C, 6])
        mv1 = sb("mv1", [P, B, C, 2])
        rs1 = sb("rs1", [P, B, C])
        nb1 = sb("nb1", [P, B, C])
        q_tok = sb("q_tok", [P, 2, C, D])
        st2 = sb("st2", [P, 2, C, 6])
        mv2 = sb("mv2", [P, 2, C, 2])
        rs2 = sb("rs2", [P, 2, C])
        nb2 = sb("nb2", [P, 2, C])
        minus1 = sb("minus1", [P, C])
        k_wt = sb("k_wt", [P, C - 1, D])
        d_sb = sb("d_sb", [P, 2, S])
        p_sb = sb("p_sb", [P, PS, S])
        state = sb("state", [P, HG, C - 1, GV])
        state2 = sb("state2", [P, 2, HG, C - 1, GV], BF16)
        carried = sb("carried", [P, C - 1, GV])
        h_sum = sb("h_sum", [P, C, NH, DV])
        norm = sb("norm", [P, 3, C, NH])
        h_n = sb("h_n", [P, C, D])
        zeros_c = h_n[:, 0].bitcast(BF16)
        lo_rows = p_sb[0:NBH, 0:2]
        relu_z = q_tok[:, :, :, :].rearrange("p a c d -> p a (c d)").rearrange("p a (h s) -> p a h s", h=KC)
        values = vaug[:].rearrange("p b c h d -> p (b c h d)")
        sq = values[:, 0:KC * S].rearrange("p (h s) -> p h s", h=KC)
        sq_hi, sq_lo = (values[:, i * KC * S:(i + 1) * KC * S].bitcast(BF16)
                        .rearrange("p (t h s) -> p t h s", t=2, h=KC) for i in (1, 2))
        logits = sb("logits", [P, B * C, E])
        biased = sb("biased", [P, B * C, E])
        lead, tied = (t[:, 0:2].rearrange("p a s -> p (a s)").rearrange("p (t n) -> p t n", t=B * C)
                          for t in (d_sb, p_sb))
        rank = sb("rank", [P, B * C, E])
        probs = sb("probs", [P, B * C, E])
        total = sb("total", [P, B * C])
        weight = sb("weight", [P, B * C, NE])

        bank = [es.enter_context(nc.psum_tensor(f"bank{i}", [P, 512], F32)) for i in range(8)]

        l_x = [sem(f"l_x{b}") for b in range(B)]
        l_kT = [sem(f"l_kT{b}") for b in range(B)]
        l_ctx = [sem(f"l_ctx{b}") for b in range(B)]
        l_w = [sem(f"l_w{i}") for i in range(3)]
        l_gate, l_bias, l_consts, l_route = sem("l_gate"), sem("l_bias"), sem("l_consts"), sem("l_route")
        stored = sem("stored")
        g_step = sem("g_step")
        ident_ok, const_ok, ones_ok = sem("ident_ok"), sem("const_ok"), sem("ones_ok")
        before_ok = sem("before_ok")
        tanh_ok, gain_ok = sem("tanh_ok"), sem("gain_ok")
        pad_ok = sem("pad_ok")
        v_step = sem("v_step")
        mv1_ok, var1_ok, rs1_ok, q_ok, qT_psum = (sem(n) for n in ("mv1_ok", "var1_ok", "rs1_ok", "q_ok", "qT_psum"))
        gates_ok, f_abs_ok, f_exp_ok, f_log_ok, a_ok, r1_ok, mid_ok, am3_ok = (
            sem(n) for n in ("gates_ok", "f_abs_ok", "f_exp_ok", "f_log_ok", "a_ok", "r1_ok", "mid_ok", "am3_ok"))
        m_ok, state_row_ok, rows_ok, rows_psum, ex_ok = (sem(n) for n in ("m_ok", "state_row_ok", "rows_ok", "rows_psum", "ex_ok"))
        decay_row_ok, decay_exp_ok, decay_psum, decay_ok = (sem(n) for n in ("decay_row_ok", "decay_exp_ok", "decay_psum", "decay_ok"))
        ones_v_ok, zero_ok, sel_ok = sem("ones_v_ok"), sem("zero_ok"), sem("sel_ok")
        k_hi_ok, q_hi_ok, q_lo_ok, neg1_ok, decay_wide_ok, gate_lo_ok, head_rows_ok = (
            sem(n) for n in ("k_hi_ok", "q_hi_ok", "q_lo_ok", "neg1_ok", "decay_wide_ok", "gate_lo_ok", "head_rows_ok"))
        k_lo_ok = [sem(f"k_lo_ok{b}") for b in range(B)]
        am_hi_ok, am_rest_ok, neg_m_ok = sem("am_hi_ok"), sem("am_rest_ok"), sem("neg_m_ok")
        zero2_ok = sem("zero2_ok")
        l_pad = [sem(f"l_pad{h}") for h in range(HG)]
        state_hi_ok, state_lo_ok, negA_ok, negB_ok = (
            sem(n) for n in ("state_hi_ok", "state_lo_ok", "negA_ok", "negB_ok"))
        k_wt_ok, d_ok, exp_ok, qk_ok, p_ok, pv_ok = (
            sem(n) for n in ("k_wt_ok", "d_ok", "exp_ok", "qk_ok", "p_ok", "pv_ok"))
        local_ok, masked_ok, carry_ok, state_ok, inter_ok, scaled_ok, comb_ok = (
            sem(n) for n in ("local_ok", "masked_ok", "carry_ok", "state_ok", "inter_ok", "scaled_ok", "comb_ok"))
        n0_ok, n1_ok, n2_ok, n3_ok, hn_ok, stA_ok, mvA_ok, varA_ok, rsA_ok, hl_ok, gained_ok, x1_ok = (
            sem(n) for n in ("n0_ok", "n1_ok", "n2_ok", "n3_ok", "hn_ok", "stA_ok", "mvA_ok", "varA_ok", "rsA_ok", "hl_ok", "gained_ok", "x1_ok"))
        stB_ok, mvB_ok, varB_ok, rsB_ok, xn_ok = (sem(n) for n in ("stB_ok", "mvB_ok", "varB_ok", "rsB_ok", "xn_ok"))
        w_hi_ok, w_ok = sem("w_hi_ok"), sem("w_ok")
        xT_psum, xT_hi_ok, xT_f_ok, xT_lo_ok = sem("xT_psum"), sem("xT_hi_ok"), sem("xT_f_ok"), sem("xT_lo_ok")
        biased_ok, lead_ok = sem("biased_ok"), sem("lead_ok")
        logit_psum, logit_ok, sel_exp_ok = (
            sem(n) for n in ("logit_psum", "logit_ok", "sel_exp_ok"))
        up_ok, relu_ok, hi_ok, sq_ok, lo_ok, down_ok, acc_ok = (
            sem(n) for n in ("up_ok", "relu_ok", "hi_ok", "sq_ok", "lo_ok", "down_ok", "acc_ok"))

        block = es.enter_context(nc.Block())

        @block.sync
        def _(sp):
            def load_x(b):
                sp.dma_start(x_all[:, b], x[b].rearrange("(c p) d -> p c d", p=P)).then_inc(l_x[b], 16)

            def load_kT(b):
                sp.dma_start(kT_stage[:, b], ctxT[b].rearrange("(k p) s -> p k s", p=P)).then_inc(l_kT[b], 16)

            def load_expert(b, i):
                sp.dma_start(w_stage[:, i], experts[:, 3 * (b - 1) + i]).then_inc(l_w[i], 16)

            load_x(0)
            sp.dma_start(gate_raw[:], gate_w.rearrange("p j (g h) -> p j g h", g=2)).then_inc(l_gate, 16)
            sp.dma_start(consts[:], row.to_broadcast([P, D + E + 2])).then_inc(l_consts, 16)
            load_kT(0)
            sp.dma_start(gate_bias[:], gate_b).then_inc(l_bias, 16)
            for b in range(1, B):
                load_x(b)
                load_kT(b)
            for b in range(B):
                for c in range(C):
                    sp.dma_start(vaug[:, b, c, :, 0:DH], ctx[b, c * P:(c + 1) * P, :].rearrange("p (h d) -> p h d", h=NH))\
                        .then_inc(l_ctx[b], 16)
            for i in range(3):
                load_expert(1, i)
            sp.dma_start(route[:], route_w).then_inc(l_route, 16)

            def pad_group(b, hg):
                for h in range(4):
                    r = h * DH
                    sp.dma_start(q_pad[r:r + DH, :, hg * 4 + h, :], qT2[r:r + DH, :, b, hg, :]).then_inc(l_pad[hg], 16)

            sp.wait_ge(zero_ok, 1)
            sp.wait_ge(zero2_ok, 1)
            sp.wait_ge(q_hi_ok, KC)
            sp.wait_ge(q_lo_ok, KC)
            pad_group(0, 0)
            pad_group(0, 1)
            sp.wait_ge(q_hi_ok, KC * B)
            sp.wait_ge(q_lo_ok, KC * B)

            def next_group(b, hg):
                sp.wait_ge(qk_ok, (b - 1) * NH + 4 * (hg + 1))
                pad_group(b, hg)

            next_group(1, 0)
            next_group(1, 1)
            with sp.Fori(2, B) as b:
                next_group(b, 0)
                for i in range(3):
                    if i == 2:
                        next_group(b, 1)
                    sp.wait_ge(w_ok, 3 * (b - 2) + i + 2)
                    load_expert(b, i)
            for b in range(B):
                sp.wait_ge(acc_ok, (NE - 1) * B + b + 1)
                sp.dma_start(out[b].rearrange("(c p) d -> p c d", p=P), x_all[:, b]).then_inc(stored, 16)
            sp.wait_ge(stored, 16 * B)

        @block.gpsimd
        def _(gp):
            g = nc.gpsimd
            g.memset(ident[:], 0.0).then_inc(g_step, 1)
            gp.wait_ge(g_step, 1)
            g.affine_select(out=ident[:], in_=ident[:], compare_op=ALU.not_equal, fill=1.0, base=0,
                            pattern=[[-1, P]], channel_multiplier=1).then_inc(ident_ok, 1)
            g.memset(eps_c[:], LN_EPS)
            g.memset(minus1[:], -1.0)
            g.memset(neg_half[:], -0.5).then_inc(g_step, 1)
            gp.wait_ge(g_step, 2)

            def rsqrt(mv, rs, nb, var_ok, neg_ok, n, done):
                g.tensor_tensor(mv[:, :, 1], mv[:, :, 1], eps_c[:], ALU.add)
                g.tensor_tensor(mv[:, :, 0], mv[:, :, 0], minus1[:], ALU.mult).then_inc(var_ok, 1)
                gp.wait_ge(var_ok, n)
                g.tensor_tensor(rs, mv[:, :, 1], neg_half[:], ALU.pow).then_inc(neg_ok, 1)
                gp.wait_ge(neg_ok, n)
                g.tensor_tensor(nb, mv[:, :, 0], rs, ALU.mult).then_inc(done, 1)

            def rsqrt_x(b):
                gp.wait_ge(mv1_ok, b + 1)
                rsqrt(mv1[:, b], rs1[:, b], nb1[:, b], var1_ok, neg1_ok, b + 1, rs1_ok)

            g.memset(gate_pad[:], 0.0).then_inc(g_step, 1)
            gp.wait_ge(l_gate, 16)
            g.tensor_copy(gate_sum[:, 0:KC], gate_raw[:, 0:KC])
            g.tensor_add(gate_sum[:, KC:], gate_raw[:, KC:2 * KC], gate_raw[:, 2 * KC:]).then_inc(g_step, 1)
            gp.wait_ge(g_step, 4)
            flat = gate_sum[:].rearrange("p k g h -> p k (g h)")
            g.tensor_copy(gate_part[:, 0], flat).then_inc(g_step, 1)
            rsqrt_x(0)
            gp.wait_ge(g_step, 5)
            g.tensor_tensor(gate_part[:, 1], flat, gate_part[:, 0], ALU.subtract).then_inc(g_step, 1)
            gp.wait_ge(g_step, 6)
            for b in range(B):
                for gate in range(2):
                    at = gate * NBH + b * NH
                    last = g.tensor_copy(gate_pad[:, b, :, :, at:at + NH],
                                         gate_part[:, :, :, gate * NH:(gate + 1) * NH].rearrange("p t k h -> p k t h"))
                if b == 1:
                    rsqrt_x(1)
            last.then_inc(pad_ok, 1)

            def k_low(b):
                gp.wait_ge(k_hi_ok, 1)
                g.tensor_tensor(kT2[:, 1, b].rearrange("p k s -> p (k s)"), kT_stage[:, b].rearrange("p k s -> p (k s)"),
                                kT2[:, 0, b].rearrange("p k s -> p (k s)"), ALU.subtract).then_inc(k_lo_ok[b], 1)

            rsqrt_x(2)
            k_low(1)
            rsqrt_x(3)
            g.memset(q_pad[:, 1].rearrange("p h s -> p (h s)").bitcast(F32), 0.0).then_inc(zero2_ok, 1)
            g.memset(zeros_c, 0.0).then_inc(g_step, 1)
            g.memset(pick3[:], 0.0).then_inc(g_step, 1)
            gp.wait_ge(g_step, 8)
            for q in range(3):
                g.affine_select(out=pick3[:], in_=pick3[:], compare_op=ALU.not_equal, fill=1.0,
                                base=-NBH * q, pattern=[[-1, NBH]], channel_multiplier=1).then_inc(g_step, 1)
                gp.wait_ge(g_step, 9 + q)
            g.memset(ones_row[:], 1.0).then_inc(ones_ok, 1)
            g.affine_select(out=mask[:], in_=zeros_c.rearrange("p (c s) -> p c s", c=C),
                            compare_op=ALU.is_ge, fill=NEG, base=0,
                            pattern=[[0, C], [1, P]], channel_multiplier=-1).then_inc(const_ok, 1)
            g.tensor_copy(ident_b[:], ident[:]).then_inc(const_ok, 1)
            g.memset(block_mask[:], SCALE).then_inc(g_step, 1)
            gp.wait_ge(g_step, 12)
            blocks = block_mask[:].rearrange("p (h d) -> p h d", h=4)
            g.affine_select(out=blocks, in_=blocks, compare_op=ALU.is_ge, fill=0.0, base=0,
                            pattern=[[-DH, 4], [0, DV]], channel_multiplier=1).then_inc(g_step, 1)
            gp.wait_ge(g_step, 13)
            g.affine_select(out=blocks, in_=blocks, compare_op=ALU.is_ge, fill=0.0, base=DH - 1,
                            pattern=[[DH, 4], [0, DV]], channel_multiplier=-1).then_inc(const_ok, 1)
            g.memset(vaug[:, :, :, :, DH:DV].rearrange("p b c h o -> p (b c h) o"), 1.0).then_inc(ones_v_ok, 1)
            gp.wait_ge(am_hi_ok, 1)
            g.tensor_tensor(am_rest[:, 0], am[:, 0], am3[0:32, 0], ALU.subtract).then_inc(am_rest_ok, 1)
            gp.wait_ge(neg_m_ok, 1)
            g.tensor_tensor(rows[0:32].rearrange("p (c s) -> p c s", c=C),
                            am[:, 0].rearrange("p (c s) -> p c s", c=C),
                            am[:, 1].rearrange("p (c s) -> p c s", c=C)[:, :, P - 1:P].to_broadcast([NBH, C, P]),
                            ALU.add).then_inc(state_row_ok, 1)

            def weigh_keys(b):
                if not isinstance(b, int) or b > 0:
                    gp.wait_ge(local_ok, b * HG)
                g.tensor_tensor(k_wt[:].rearrange("p c (h d) -> p c h d", h=NH),
                                vaug[:, b, 0:C - 1, :, 0:DH],
                                ex[:, 0:C - 1, bass.ds(b * NH, NH)].unsqueeze(3).to_broadcast([P, C - 1, NH, DH]),
                                ALU.mult).then_inc(k_wt_ok, 1)

            def attention_norm(t):
                gp.wait_ge(mvA_ok, t + 1)
                rsqrt(mv2[:, 0], rs2[:, 0], nb2[:, 0], varA_ok, negA_ok, t + 1, rsA_ok)

            def add_residual(t):
                for half in range(2):
                    n = 2 * t + half + 1
                    at = slice(2 * half, 2 * half + 2)
                    gp.wait_ge(hl_ok, n)
                    g.tensor_tensor(h_n[:, at], h_n[:, at], ln_gain[:].unsqueeze(1).to_broadcast([P, 2, D]),
                                    ALU.mult).then_inc(gained_ok, 1)
                    gp.wait_ge(gained_ok, n)
                    g.tensor_tensor(x_all[:, t, at].rearrange("p c d -> p (c d)"),
                                    x_all[:, t, at].rearrange("p c d -> p (c d)"),
                                    h_n[:, at].rearrange("p c d -> p (c d)"), ALU.add).then_inc(x1_ok, 1)

            def expert_norm(t):
                if t > 0:
                    gp.wait_ge(xn_ok, t)
                gp.wait_ge(mvB_ok, t + 1)
                rsqrt(mv2[:, 1], rs2[:, 1], nb2[:, 1], varB_ok, negB_ok, t + 1, rsB_ok)

            def low_part(b, i):
                e = 3 * (b - 1) + i
                gp.wait_ge(w_hi_ok, e + 1)
                g.tensor_tensor(w_lo[:, e].rearrange("p a k d -> p (a k d)"),
                                w_stage[:, i].rearrange("p a k d -> p (a k d)"),
                                w_hi[:, e].rearrange("p a k d -> p (a k d)"), ALU.subtract).then_inc(w_ok, 1)

            gp.wait_ge(ex_ok, 1)
            gp.wait_ge(l_ctx[0], 16 * C)
            weigh_keys(0)
            g.memset(before[:], 1.0).then_inc(g_step, 1)
            gp.wait_ge(g_step, 14)
            g.affine_select(out=before[:], in_=before[:], compare_op=ALU.is_gt, fill=0.0, base=0,
                            pattern=[[1, E], [-1, E]], channel_multiplier=0).then_inc(before_ok, 1)
            g.memset(total[:], 0.0).then_inc(w_ok, 1)
            gp.wait_ge(gain_ok, 1)
            gp.wait_ge(am3_ok, 1)
            gp.wait_ge(mid_ok, 1)
            gp.wait_ge(l_ctx[1], 16 * C)
            weigh_keys(1)
            for b in range(1, B):
                if b > 1:
                    expert_norm(b - 2)
                low_part(b, 0)
                low_part(b, 1)
                attention_norm(b - 1)
                if b + 1 < B:
                    gp.wait_ge(l_ctx[b + 1], 16 * C)
                    weigh_keys(b + 1)
                add_residual(b - 1)
                low_part(b, 2)

            def low_x(b):
                gp.wait_ge(xT_f_ok, KC * (b + 1))
                g.tensor_tensor(xT_lo[:, b].rearrange("p k s -> p (k s)"), xT[:, b].rearrange("p k s -> p (k s)"),
                                xT_hi[:, b].rearrange("p k s -> p (k s)"), ALU.subtract).then_inc(xT_lo_ok, KC)

            gp.wait_ge(xT_lo_ok, KC)
            low_x(1)
            expert_norm(B - 2)
            attention_norm(B - 1)
            low_x(2)
            expert_norm(B - 1)

            def compare(n, at):
                count = len(range(C * B)[at])
                gp.wait_ge(logit_ok, n + 1)
                g.tensor_tensor(biased[:, at], logits[:, at],
                                consts[:, D:D + E].unsqueeze(1).to_broadcast([P, count, E]), ALU.add).then_inc(biased_ok, 1)
                gp.wait_ge(biased_ok, n + 1)
                g.tensor_tensor(lead[:, at].rearrange("p t (j i) -> p t j i", j=E),
                                biased[:, at].unsqueeze(2).to_broadcast([P, count, E, E]),
                                biased[:, at].unsqueeze(3).to_broadcast([P, count, E, E]), ALU.subtract).then_inc(lead_ok, 1)

            compare(0, slice(0, 3 * C))
            low_x(B - 1)
            compare(1, slice(3 * C, B * C))

        @block.tensor
        def _(pe):
            mm = nc.tensor.matmul

            def transpose_q(b):
                if b >= 2:
                    pe.wait_ge(q_lo_ok, KC * (b - 1))
                pe.wait_ge(q_ok, b + 1)
                for k in range(KC):
                    for c in range(C):
                        last = nc.tensor.transpose(bank[2 + 2 * (b % 2) + k][:, c * P:(c + 1) * P],
                                                   q_tok[:, b % 2, c, k * P:(k + 1) * P], ident[:])
                    last.then_inc(qT_psum, 1)

            def gates(b, half, data):
                for k in range(KC):
                    for part in range(2):
                        last = mm(bank[0][:], gate_pad[:, b, half + k].rearrange("p t m -> p (t m)"), data[:, part, b, k, :],
                                  start=(b == 0 and half == KC and k + part == 0),
                                  stop=(b == B - 1 and half == 0 and k + part == KC))
                return last

            def gates_q(b):
                pe.wait_ge(q_lo_ok, KC * (b + 1))
                return gates(b, 0, qT2)

            def gates_ctx(b):
                pe.wait_ge(k_lo_ok[b], 1)
                gates(b, KC, kT2)

            pe.wait_ge(ident_ok, 1)
            transpose_q(0)
            pe.wait_ge(pad_ok, 1)
            gates_ctx(0)
            for b in range(1, B):
                transpose_q(b)
                if b < B - 1:
                    gates_ctx(b)
                if b == B - 2:
                    gates_ctx(B - 1)
                gates_q(b - 1)
            gates_q(B - 1).then_inc(gates_ok, 1)

            def head_scores(b, j):
                n = b * NH + j
                free = not isinstance(b, int) or n >= 2
                if free:
                    pe.wait_ge(exp_ok, n - 1)
                pick = pick3[:, bass.ds(n, 1)].to_broadcast([96, P])
                mm(bank[j % 2][:], pick, am3[:, 1, :], start=True, stop=False)
                for c in range(C):
                    mm(bank[j % 2][:, c * P:(c + 1) * P], am3[:, 0, c * P:(c + 1) * P], pick,
                       start=False, stop=False)
                mm(bank[j % 2][:], ident_b[:], mask[:].rearrange("p c s -> p (c s)"),
                   start=False, stop=True).then_inc(d_ok, 1)
                if j % 4 == 0:
                    pe.wait_ge(l_pad[j // 4], 64 * (b + 1))
                if free:
                    pe.wait_ge(p_ok, n - 1)
                for c in range(C):
                    at = slice(c * P, (c + 1) * P)
                    for m, (kp, qp) in enumerate(((0, 0), (0, 1), (1, 0))):
                        last = mm(bank[2 + j % 2][:, at], kT2[:, kp, b, j // 4, at], q_pad[:, qp, j, at],
                                  start=(m == 0), stop=(m == MIXED - 1))
                last.then_inc(qk_ok, 1)

            def head_values(b, j):
                n = b * NH + j
                pe.wait_ge(p_ok, n + 1)
                if j % 4 == 0 and (not isinstance(b, int) or n > 0):
                    pe.wait_ge(comb_ok, b * HG + j // 4)
                for c in range(C):
                    at = (c % 2) * GV + (j % 4) * DV
                    last = mm(bank[4 + c // 2][:, at:at + DV], p_sb[:, j % PS, c * P:(c + 1) * P],
                              vaug[:, b, c, j, :], start=True, stop=True)
                last.then_inc(pv_ok, 1)

            def group_state(b, hg):
                if hg == 0:
                    pe.wait_ge(k_wt_ok, b + 1)
                if isinstance(b, int) and b + hg == 0:
                    pe.wait_ge(decay_ok, 1)
                    pe.wait_ge(ones_v_ok, 1)
                    pe.wait_ge(l_ctx[0], 16 * C)
                if not isinstance(b, int) or b + hg > 0:
                    pe.wait_ge(masked_ok, b * HG + hg)
                for c in range(C - 1):
                    last = mm(bank[7][:, c * GV:(c + 1) * GV], k_wt[:, c, hg * P:(hg + 1) * P],
                              vaug[:, b, c, hg * 4:hg * 4 + 4, :].rearrange("p h d -> p (h d)"), start=True, stop=True)
                last.then_inc(local_ok, 1)

            def group_inter(b, hg):
                pe.wait_ge(state_lo_ok, b * HG + hg + 1)
                if not isinstance(b, int) or b + hg > 0:
                    pe.wait_ge(comb_ok, b * HG + hg)
                for c in range(1, C):
                    for m, (qp, part) in enumerate(((0, 0), (0, 1), (1, 0))):
                        last = mm(bank[6][:, (c - 1) * GV:c * GV], qT2[:, qp, b, hg, c * P:(c + 1) * P],
                                  state2[:, part, hg, c - 1, :], start=(m == 0), stop=(m == MIXED - 1))
                last.then_inc(inter_ok, 1)

            def batch(b, first):
                for j in range(NH):
                    head_scores(b, j)
                    if j % 4 == 0:
                        group_state(b, j // 4)
                    if j >= LAG:
                        head_values(b, j - LAG)
                    elif not first:
                        head_values(b - 1, NH + j - LAG)
                    if j % 4 == 3:
                        group_inter(b, j // 4)

            pe.wait_ge(rows_ok, 1)
            pe.wait_ge(state_row_ok, 1)
            for c in range(C):
                last = nc.tensor.transpose(bank[5][:, c * 96:(c + 1) * 96], rows[:, c * P:(c + 1) * P],
                                           ident[0:96, 0:96])
            last.then_inc(rows_psum, 1)
            pe.wait_ge(decay_wide_ok, 1)
            pe.wait_ge(head_rows_ok, 1)
            mm(bank[7][:, 0:4 * B], head_rows[:],
               decay_wide[:].rearrange("r n t -> r (n t)"), start=True, stop=True).then_inc(decay_psum, 1)
            pe.wait_ge(const_ok, 3)
            pe.wait_ge(am3_ok, 1)
            pe.wait_ge(mid_ok, 1)
            pe.wait_ge(am_hi_ok, 2)
            batch(0, True)
            for b in range(1, B):
                pe.wait_ge(l_ctx[b], 16 * C)
            with pe.Fori(1, B) as b:
                batch(b, False)

            def transpose_x(b):
                lo = 2 * (b % 2)
                pe.wait_ge(xn_ok, b + 1)
                for k in range(KC):
                    for c in range(C):
                        last = nc.tensor.transpose(bank[lo + k][:, c * P:(c + 1) * P],
                                                   xn[:, b, c, k * P:(k + 1) * P], ident[:])
                    last.then_inc(xT_psum, 1)

            def router(b, to, at):
                pe.wait_ge(xT_f_ok, KC * (b + 1))
                for c in range(C):
                    for k in range(KC):
                        last = mm(to[:, at + c * E:at + (c + 1) * E], xT[:, b, k, c * P:(c + 1) * P], route[:, k, :],
                                  start=(k == 0), stop=(k == KC - 1))
                last.then_inc(logit_psum, 1)

            def up(e, b):
                n = e * B + b
                if b == 0:
                    pe.wait_ge(w_ok, e + 2)
                if not isinstance(n, int) or n >= 2:
                    pe.wait_ge(relu_ok, KC * (n - 1))
                for h in range(KC):
                    for k in range(KC):
                        for m, (w, xx) in enumerate(((w_hi, xT_hi), (w_hi, xT_lo), (w_lo, xT_hi))):
                            last = mm(bank[2 * (b % 2) + h][:], w[:, e, 0, k, h * P:(h + 1) * P], xx[:, b, k, :],
                                      start=(k == 0 and m == 0), stop=(k == KC - 1 and m == MIXED - 1))
                    last.then_inc(up_ok, 1)

            def down(e, b):
                n = e * B + b
                pe.wait_ge(hi_ok, KC * (n + 1))
                pe.wait_ge(lo_ok, KC * (n + 1))
                if not isinstance(n, int) or n >= 2:
                    pe.wait_ge(acc_ok, n - 1)
                for c in range(C):
                    for h in range(KC):
                        for m, (s, w) in enumerate(((sq_hi, w_hi), (sq_hi, w_lo), (sq_lo, w_hi))):
                            at = (c % 2) * D
                            last = mm(bank[4 + 2 * (b % 2) + c // 2][:, at:at + D],
                                      s[:, b % 2, h, c * P:(c + 1) * P], w[:, e, 1, h, :],
                                      start=(h == 0 and m == 0), stop=(h == KC - 1 and m == MIXED - 1))
                last.then_inc(down_ok, 1)

            def split_x(b):
                pe.wait_ge(xT_hi_ok, KC * (b + 1))
                pe.wait_ge(xT_lo_ok, KC * (b + 1))

            pe.wait_ge(exp_ok, B * NH)
            transpose_x(0)
            head_values(B - 1, NH - 2)
            head_values(B - 1, NH - 1)
            pe.wait_ge(p_ok, B * NH)
            transpose_x(1)
            split_x(0)
            up(0, 0)
            split_x(1)
            up(0, 1)
            pe.wait_ge(comb_ok, HG * B)
            pe.wait_ge(relu_ok, KC)
            transpose_x(2)
            down(0, 0)
            down(0, 1)
            pe.wait_ge(l_route, 16)
            split_x(2)
            up(0, 2)
            pe.wait_ge(acc_ok, 1)
            for b in range(3):
                router(b, bank[4], b * C * E)
            transpose_x(3)
            pe.wait_ge(logit_ok, 1)
            down(0, 2)
            pe.wait_ge(acc_ok, 2)
            router(3, bank[6], 0)
            split_x(3)
            up(0, 3)
            pe.wait_ge(logit_ok, 2)
            with pe.Fori(1, NE) as e:
                up(e, 0)
                down(e - 1, B - 1)
                for b in range(1, B):
                    up(e, b)
                    down(e, b - 1)
            down(NE - 1, B - 1)

        @block.scalar
        def _(act):
            s = nc.scalar
            act.wait_ge(l_consts, 16)
            s.activation(tanhs[:], consts[:, D + E:D + E + 2], ACT.Tanh).then_inc(tanh_ok, 1)
            s.preload_act_table_set("natural_log_exp_and_others")

            def normalise(to, data, rs, nb, done, chunks=range(C)):
                for c in chunks:
                    last = s.activation(to[:, c, :], data[:, c, :], ACT.Identity, bias=nb[:, c:c + 1], scale=rs[:, c:c + 1])
                if done is not None:
                    last.then_inc(done, 1)

            def normalise_x(b):
                act.wait_ge(rs1_ok, b + 1)
                if b >= 2:
                    act.wait_ge(qT_psum, KC * (b - 1))
                normalise(q_tok[:, b % 2], x_all[:, b], rs1[:, b], nb1[:, b], q_ok)

            def high_k(b):
                act.wait_ge(l_kT[b], 16)
                s.activation(kT2[:, 0, b].rearrange("p k s -> p (k s)"), kT_stage[:, b].rearrange("p k s -> p (k s)"),
                             ACT.Copy).then_inc(k_hi_ok, 1)

            normalise_x(0)
            for b in range(B):
                if b == 0:
                    high_k(1)
                if b + 1 < B:
                    normalise_x(b + 1)
                for k in range(KC):
                    act.wait_ge(qT_psum, KC * b + k + 1)
                    s.activation(qT2[:, 0, b, k, :], bank[2 + 2 * (b % 2) + k][:], ACT.Copy).then_inc(q_hi_ok, 1)
            act.wait_ge(gates_ok, 1)
            for gate in (1, 0):
                at = 2 * NBH + gate * NBH
                s.activation(lo_rows[:, gate], bank[0][at:at + NBH, :], ACT.Copy).then_inc(gate_lo_ok, 1)
            act.wait_ge(f_abs_ok, 1)
            s.activation(f_abs, f_abs, ACT.Exp, scale=-1.0).then_inc(f_exp_ok, 1)
            act.wait_ge(f_exp_ok, 1)
            s.activation(f_abs, f_abs, ACT.Ln, bias=1.0).then_inc(f_log_ok, 1)
            act.wait_ge(a_ok, 1)
            s.activation(am3[0:32, 0], am[:, 0], ACT.Copy).then_inc(am_hi_ok, 1)
            act.wait_ge(m_ok, 1)
            s.activation(am[:, 1], f_pre, ACT.Copy, scale=-1.0).then_inc(neg_m_ok, 1)
            act.wait_ge(neg_m_ok, 1)
            s.activation(am3[0:32, 1], am[:, 1], ACT.Copy).then_inc(am_hi_ok, 1)
            act.wait_ge(am_rest_ok, 1)
            act.wait_ge(r1_ok, 1)
            s.activation(am3[32:64], am_rest, ACT.Copy).then_inc(mid_ok, 1)
            act.wait_ge(decay_row_ok, 1)
            s.activation(decay_exp[:], decay_row[:], ACT.Exp).then_inc(decay_exp_ok, 1)
            act.wait_ge(rows_psum, 1)
            s.activation(ex[:].rearrange("p c r -> p (c r)"), bank[5][:, 0:C * 96], ACT.Exp).then_inc(ex_ok, 1)
            act.wait_ge(decay_psum, 1)
            s.activation(decay[:].rearrange("p n t -> p (n t)"), bank[7][:, 0:4 * B], ACT.Copy).then_inc(decay_ok, 1)

            def head_exp(b, j):
                n = b * NH + j
                act.wait_ge(d_ok, n + 1)
                if not isinstance(b, int) or n >= 2:
                    act.wait_ge(p_ok, n - 1)
                s.activation(d_sb[:, j % 2, :], bank[j % 2][:], ACT.Exp).then_inc(exp_ok, 1)

            def high_part(b, i):
                e = 3 * (b - 1) + i
                act.wait_ge(l_w[i], 16 * b)
                s.activation(w_hi[:, e].rearrange("p a k d -> p (a k d)"),
                             w_stage[:, i].rearrange("p a k d -> p (a k d)"), ACT.Copy).then_inc(w_hi_ok, 1)

            def state_high(b, hg):
                n = b * HG + hg
                act.wait_ge(state_ok, n + 1)
                if not isinstance(b, int) or b > 0:
                    act.wait_ge(inter_ok, n - 1)
                s.activation(state2[:, 0, hg], state[:, hg], ACT.Copy).then_inc(state_hi_ok, 1)

            def normaliseA(t, half):
                if half == 0:
                    act.wait_ge(rsA_ok, t + 1)
                normalise(h_n[:], h_n[:], rs2[:, 0], nb2[:, 0], hl_ok, (2 * half, 2 * half + 1))

            def normaliseB(t, half):
                if half == 0:
                    act.wait_ge(rsB_ok, t + 1)
                normalise(xn[:, t], x_all[:, t], rs2[:, 1], nb2[:, 1], xn_ok if half else None, (2 * half, 2 * half + 1))

            def batch(b, before):
                for j in range(NH):
                    head_exp(b, j)
                    if j % 4 == 1:
                        state_high(b, j // 4)
                    if before and j in (0, 2, 4):
                        high_part(b, j // 2)
                    if before > 1 and j in (3, 7):
                        normaliseB(b - 2, j // 4)
                    if before and j in (5, 6):
                        normaliseA(b - 1, j - 5)

            batch(0, 0)
            batch(1, 1)
            with act.Fori(2, B) as b:
                batch(b, 2)

            def copy_x(b):
                lo = 2 * (b % 2)
                for k in range(KC):
                    act.wait_ge(xT_psum, KC * b + k + 1)
                    s.activation(xT_hi[:, b, k, :], bank[lo + k][:], ACT.Copy).then_inc(xT_hi_ok, 1)
                    s.activation(xT[:, b, k, :], bank[lo + k][:], ACT.Copy).then_inc(xT_f_ok, 1)

            def relu(e, b):
                n = e * B + b
                for h in range(KC):
                    act.wait_ge(up_ok, KC * n + h + 1)
                    if not isinstance(n, int) or n >= 2:
                        act.wait_ge(sq_ok, KC * (n - 2) + h + 1)
                    s.activation(relu_z[:, b % 2, h, :], bank[2 * (b % 2) + h][:], ACT.Relu).then_inc(relu_ok, 1)
                for h in range(KC):
                    act.wait_ge(relu_ok, KC * n + h + 1)
                    if not isinstance(n, int) or n >= 2:
                        act.wait_ge(down_ok, n - 1)
                    s.activation(sq_hi[:, b % 2, h, :], relu_z[:, b % 2, h, :], ACT.Square).then_inc(hi_ok, 1)

            copy_x(0)
            copy_x(1)
            relu(0, 0)
            normaliseB(B - 2, 0)
            normaliseB(B - 2, 1)
            relu(0, 1)
            copy_x(2)
            normaliseA(B - 1, 0)
            normaliseA(B - 1, 1)

            def copy_logits(n, bank_of, chunks):
                count = len(range(C * B)[chunks])
                act.wait_ge(logit_psum, 3 if n == 1 else 4)
                s.activation(logits[:, chunks].rearrange("p t e -> p (t e)"), bank_of[:, 0:count * E],
                             ACT.Copy).then_inc(logit_ok, 1)
                act.wait_ge(logit_ok, n)
                s.activation(probs[:, chunks], logits[:, chunks], ACT.Exp, scale=-1.0).then_inc(sel_exp_ok, 1)

            relu(0, 2)
            normaliseB(B - 1, 0)
            normaliseB(B - 1, 1)
            copy_logits(1, bank[4], slice(0, 3 * C))
            copy_x(3)
            copy_logits(2, bank[6], slice(3 * C, B * C))
            relu(0, 3)
            with act.Fori(1, NE) as e:
                for b in range(B):
                    relu(e, b)

        @block.vector
        def _(dve):
            v = nc.vector
            steps = [0]

            def step(ins):
                steps[0] += 1
                ins.then_inc(v_step, 1)
                dve.wait_ge(v_step, steps[0])

            def stats(b):
                dve.wait_ge(l_x[b], 16)
                for c in range(C):
                    last = v.bn_stats(st1[:, b, c, :], x_all[:, b, c, :])
                step(last)
                for c in range(C):
                    last = v.bn_aggr(mv1[:, b, c, :], st1[:, b, c, :])
                last.then_inc(mv1_ok, 1)

            def low_q(b):
                for k in range(KC):
                    dve.wait_ge(q_hi_ok, KC * b + k + 1)
                    v.tensor_tensor(qT2[:, 1, b, k, :], bank[2 + 2 * (b % 2) + k][:], qT2[:, 0, b, k, :],
                                    ALU.subtract).then_inc(q_lo_ok, 1)

            dve.wait_ge(ident_ok, 1)
            v.tensor_reduce(is_head[:], ident[0:NBH, 0:NBH].rearrange("p (n h) -> p h n", h=4), AX.X, ALU.add)
            v.tensor_reduce(is_group[:], ident[0:NBH, 0:NBH].rearrange("p (n h) -> p n h", h=4), AX.X,
                            ALU.add).then_inc(sel_ok, 1)
            dve.wait_ge(sel_ok, 1)
            v.tensor_copy(head_rows[:].rearrange("r (h d) -> r h d", h=4),
                          is_head[:].unsqueeze(2).to_broadcast([NBH, 4, DH])).then_inc(head_rows_ok, 1)
            step(v.memset(rows[32:64, 0:P], 0.0))
            v.memset(q_pad[:, 0].rearrange("p h s -> p (h s)").bitcast(F32), 0.0).then_inc(zero_ok, 1)

            def split_k(b):
                flat = "p k s -> p (k s)"
                dve.wait_ge(l_kT[b], 16)
                step(v.tensor_copy(kT2[:, 0, b].rearrange(flat), kT_stage[:, b].rearrange(flat)))
                v.tensor_tensor(kT2[:, 1, b].rearrange(flat), kT_stage[:, b].rearrange(flat),
                                kT2[:, 0, b].rearrange(flat), ALU.subtract).then_inc(k_lo_ok[b], 1)

            stats(0)
            split_k(0)
            stats(1)
            stats(2)
            split_k(2)
            stats(3)
            low_q(0)
            split_k(3)
            for b in range(1, B):
                low_q(b)
            dve.wait_ge(tanh_ok, 1)
            v.tensor_scalar(ln_gain[:], consts[:, 0:D], tanhs[:, 0:1], None, ALU.mult).then_inc(gain_ok, 1)

            dve.wait_ge(gates_ok, 1)
            dve.wait_ge(l_bias, 16)
            dve.wait_ge(gate_lo_ok, 1)
            step(v.scalar_tensor_tensor(f_pre, bank[0][NBH:2 * NBH, :], gate_bias[:, 1:2], lo_rows[:, 1],
                                        ALU.add, ALU.add))
            v.scalar_tensor_tensor(f_abs, f_pre, -1.0, f_pre, ALU.mult, ALU.max).then_inc(f_abs_ok, 1)
            dve.wait_ge(gate_lo_ok, 2)
            step(v.scalar_tensor_tensor(am[:, 0], bank[0][0:NBH, :], gate_bias[:, 0:1], lo_rows[:, 0],
                                        ALU.add, ALU.add))
            dve.wait_ge(f_log_ok, 1)
            step(v.scalar_tensor_tensor(log_f, f_pre, 0.0, f_abs, ALU.min, ALU.subtract))
            dve.wait_ge(ones_ok, 1)
            step(v.tensor_tensor_scan(cs, log_f, ones_row[:], 0.0, ALU.add, ALU.mult))
            dve.wait_ge(sel_ok, 1)
            v.tensor_tensor(am[:, 0], am[:, 0], cs, ALU.subtract).then_inc(a_ok, 1)
            dve.wait_ge(a_ok, 1)
            m_row = f_pre
            m_end = m_row.rearrange("p (c s) -> p c s", c=C)[:, :, P - 1:P]
            v.tensor_tensor_scan(m_row, am[:, 0], am[:, 0], LOWEST, ALU.max, ALU.max).then_inc(m_ok, 1)
            dve.wait_ge(m_ok, 1)
            v.tensor_tensor(decay_row[:].unsqueeze(2), m_end[:, 0:2], m_end[:, 1:3], ALU.subtract)\
                .then_inc(decay_row_ok, 1)
            v.tensor_tensor(rows[32:64, P:].rearrange("p (c s) -> p c s", c=C - 1),
                            m_end[:, 0:C - 1].to_broadcast([NBH, C - 1, P]),
                            m_row[:, P:].rearrange("p (c s) -> p c s", c=C - 1), ALU.subtract)
            v.scalar_tensor_tensor(rows[64:96], cs, -1.0, m_row, ALU.mult, ALU.subtract).then_inc(rows_ok, 1)
            dve.wait_ge(am_hi_ok, 2)
            v.tensor_tensor(am_rest[:, 1], am[:, 1], am3[0:32, 1], ALU.subtract).then_inc(r1_ok, 1)
            dve.wait_ge(r1_ok, 1)
            dve.wait_ge(am_rest_ok, 1)
            step(v.tensor_copy(am_mid, am_rest))
            v.tensor_tensor(am3[64:96], am_rest, am_mid, ALU.subtract).then_inc(am3_ok, 1)
            dve.wait_ge(decay_exp_ok, 1)
            v.tensor_tensor(decay_wide[:], decay_exp[:].unsqueeze(1).to_broadcast([NBH, B * HG, 2]),
                            is_group[:].unsqueeze(2).to_broadcast([NBH, B * HG, 2]), ALU.mult).then_inc(decay_wide_ok, 1)

            def head_product(b, j):
                n = b * NH + j
                dve.wait_ge(exp_ok, n + 1)
                dve.wait_ge(qk_ok, n + 1)
                if not isinstance(b, int) or n >= PS:
                    dve.wait_ge(pv_ok, n - PS + 1)
                v.scalar_tensor_tensor(p_sb[:, j % PS, :], bank[2 + j % 2][:], SCALE, d_sb[:, j % 2, :],
                                       ALU.mult, ALU.mult).then_inc(p_ok, 1)

            def group_states(b, hg):
                n = b * HG + hg
                dve.wait_ge(local_ok, n + 1)
                if not isinstance(b, int) or b > 0:
                    dve.wait_ge(state_lo_ok, n - 1)
                v.tensor_tensor(state[:, hg], bank[7][:, 0:(C - 1) * GV].rearrange("p (c g) -> p c g", c=C - 1),
                                block_mask[:].unsqueeze(1).to_broadcast([P, C - 1, GV]), ALU.mult).then_inc(masked_ok, 1)
                dve.wait_ge(masked_ok, n + 1)
                v.scalar_tensor_tensor(state[:, hg, 1], state[:, hg, 0], decay[:, n, 0:1], state[:, hg, 1],
                                       ALU.mult, ALU.add).then_inc(carry_ok, 1)
                dve.wait_ge(carry_ok, n + 1)
                v.scalar_tensor_tensor(state[:, hg, 2], state[:, hg, 1], decay[:, n, 1:2], state[:, hg, 2],
                                       ALU.mult, ALU.add).then_inc(state_ok, 1)

            def state_low(b, hg):
                n = b * HG + hg
                dve.wait_ge(state_hi_ok, n + 1)
                v.tensor_tensor(state2[:, 1, hg], state[:, hg], state2[:, 0, hg], ALU.subtract).then_inc(state_lo_ok, 1)

            def group_combine(b, hg):
                n = b * HG + hg
                dve.wait_ge(inter_ok, n + 1)
                v.tensor_tensor(carried[:].rearrange("p c (h d) -> p c h d", h=4),
                                bank[6][:, 0:(C - 1) * GV].rearrange("p (c h d) -> p c h d", c=C - 1, h=4),
                                ex[:, 1:C, bass.ds(NBH + n * 4, 4)].unsqueeze(3).to_broadcast([P, C - 1, 4, DV]),
                                ALU.mult).then_inc(scaled_ok, 1)
                dve.wait_ge(pv_ok, (n + 1) * 4)
                h4 = h_sum[:, :, hg * 4:hg * 4 + 4, :].rearrange("p c h d -> p c (h d)")
                v.tensor_copy(h4[:, 0], bank[4][:, 0:GV])
                dve.wait_ge(scaled_ok, n + 1)
                v.tensor_tensor(h4[:, 1], bank[4][:, GV:2 * GV], carried[:, 0], ALU.add)
                v.tensor_tensor(h4[:, 2:4], bank[5][:, 0:2 * GV].rearrange("p (c g) -> p c g", c=2),
                                carried[:, 1:3], ALU.add).then_inc(comb_ok, 1)

            def norm_max(t):
                dve.wait_ge(comb_ok, HG * (t + 1))
                v.scalar_tensor_tensor(norm[:, 0], h_sum[:, :, :, DH], -1.0, ex[:, :, bass.ds(2 * NBH + t * NH, NH)],
                                       ALU.mult, ALU.max).then_inc(n0_ok, 1)

            def norm_eps(t):
                dve.wait_ge(n0_ok, t + 1)
                v.tensor_tensor(norm[:, 2], norm[:, 0], h_sum[:, :, :, DH], ALU.max).then_inc(n1_ok, 1)
                dve.wait_ge(n1_ok, t + 1)
                v.tensor_scalar(norm[:, 1], norm[:, 2], EPS, None, ALU.add).then_inc(n2_ok, 1)

            def norm_divide(t):
                if not isinstance(t, int) or t > 0:
                    dve.wait_ge(x1_ok, 2 * t)
                dve.wait_ge(n2_ok, t + 1)
                v.reciprocal(norm[:, 2], norm[:, 1]).then_inc(n3_ok, 1)
                dve.wait_ge(n3_ok, t + 1)
                v.tensor_tensor(h_n[:].rearrange("p c (h d) -> p (c h) d", h=NH),
                                h_sum[:, :, :, 0:DH].rearrange("p c h d -> p (c h) d"),
                                norm[:, 2].rearrange("p c h -> p (c h)").unsqueeze(2).to_broadcast([P, C * NH, DH]),
                                ALU.mult).then_inc(hn_ok, 1)

            def statsA(t):
                dve.wait_ge(hn_ok, t + 1)
                for c in range(C):
                    last = v.bn_stats(st2[:, 0, c, :], h_n[:, c, :])
                last.then_inc(stA_ok, 1)

            def meanA():
                for c in range(C):
                    last = v.bn_aggr(mv2[:, 0, c, :], st2[:, 0, c, :])
                last.then_inc(mvA_ok, 1)

            def statsB(t, half):
                dve.wait_ge(x1_ok, 2 * (t + 1))
                for c in (2 * half, 2 * half + 1):
                    last = v.bn_stats(st2[:, 1, c, :], x_all[:, t, c, :])
                last.then_inc(stB_ok, 1)

            def meanB():
                for c in range(C):
                    last = v.bn_aggr(mv2[:, 1, c, :], st2[:, 1, c, :])
                last.then_inc(mvB_ok, 1)

            def batch(b, before):
                for j in range(NH):
                    if before > 1 and j == 2:
                        dve.wait_ge(stB_ok, 2 * (b - 1))
                    if before and j == 4:
                        dve.wait_ge(stA_ok, b)
                    head_product(b, j)
                    if j == 0:
                        group_states(b, 0)
                        if before > 1:
                            statsB(b - 2, 0)
                    if j == 1 and before:
                        group_combine(b - 1, 1)
                        norm_max(b - 1)
                        norm_eps(b - 1)
                        if before > 1:
                            statsB(b - 2, 1)
                    if j == 2:
                        state_low(b, 0)
                        if before > 1:
                            meanB()
                        if before:
                            norm_divide(b - 1)
                    if j == 3 and before:
                        statsA(b - 1)
                    if j == 4:
                        if before:
                            meanA()
                        group_states(b, 1)
                    if j == 5:
                        group_combine(b, 0)
                    if j == 6:
                        state_low(b, 1)

            dve.wait_ge(decay_ok, 1)
            dve.wait_ge(const_ok, 3)
            dve.wait_ge(ex_ok, 1)
            batch(0, 0)
            batch(1, 1)
            with dve.Fori(2, B) as b:
                batch(b, 2)

            def low_x(b):
                lo = 2 * (b % 2)
                for k in range(KC):
                    dve.wait_ge(xT_f_ok, KC * b + k + 1)
                    v.tensor_tensor(xT_lo[:, b, k, :], bank[lo + k][:], xT_hi[:, b, k, :],
                                    ALU.subtract).then_inc(xT_lo_ok, 1)

            def square(e, b):
                n = e * B + b
                for h in range(KC):
                    dve.wait_ge(relu_ok, KC * n + h + 1)
                    if not isinstance(n, int) or n >= 1:
                        dve.wait_ge(lo_ok, KC * (n - 1) + h + 1)
                    v.tensor_tensor(sq[:, h, :], relu_z[:, b % 2, h, :], relu_z[:, b % 2, h, :],
                                    ALU.mult).then_inc(sq_ok, 1)
                for h in range(KC):
                    dve.wait_ge(sq_ok, KC * n + h + 1)
                    dve.wait_ge(hi_ok, KC * n + h + 1)
                    v.tensor_tensor(sq_lo[:, b % 2, h, :], sq[:, h, :], sq_hi[:, b % 2, h, :],
                                    ALU.subtract).then_inc(lo_ok, 1)

            def accumulate(e, b):
                n = e * B + b
                dve.wait_ge(down_ok, n + 1)
                if not isinstance(n, int) or n >= B:
                    dve.wait_ge(acc_ok, n - B + 1)
                for c in range(C):
                    at = (c % 2) * D
                    last = v.scalar_tensor_tensor(x_all[:, b, c, :], bank[4 + 2 * (b % 2) + c // 2][:, at:at + D],
                                                  weight[:, b * C + c, bass.ds(e, 1)], x_all[:, b, c, :],
                                                  ALU.mult, ALU.add)
                last.then_inc(acc_ok, 1)

            def weigh_experts(n, at):
                count = len(range(C * B)[at])
                dve.wait_ge(lead_ok, n)
                step(v.scalar_tensor_tensor(tied[:, at], lead[:, at], 0.0, before[:].rearrange("p j i -> p (j i)")
                                            .unsqueeze(1).to_broadcast([P, count, E * E]), ALU.is_equal, ALU.mult))
                step(v.scalar_tensor_tensor(lead[:, at], lead[:, at], 0.0, tied[:, at], ALU.is_gt, ALU.add))
                step(v.tensor_reduce(rank[:, at], lead[:, at].rearrange("p t (j i) -> p t j i", j=E), AX.X, ALU.add))
                dve.wait_ge(sel_exp_ok, n)
                step(v.tensor_scalar(probs[:, at], probs[:, at], 1.0, None, ALU.add))
                step(v.reciprocal(probs[:, at], probs[:, at]))
                step(v.scalar_tensor_tensor(probs[:, at], rank[:, at], 1.5, probs[:, at], ALU.is_lt, ALU.mult))
                step(v.tensor_reduce(total[:, at], probs[:, at], AX.X, ALU.add))
                step(v.tensor_scalar(total[:, at], total[:, at], W_EPS, None, ALU.add))
                step(v.reciprocal(total[:, at], total[:, at]))
                step(v.tensor_scalar(total[:, at], total[:, at], tanhs[:, 1:2], None, ALU.mult))
                step(v.tensor_tensor(weight[:, at, 1:NE], probs[:, at], total[:, at].unsqueeze(2).to_broadcast([P, count, E]),
                                     ALU.mult))

            def last_residual():
                t = B - 1
                for half in range(2):
                    at = slice(2 * half, 2 * half + 2)
                    dve.wait_ge(hl_ok, 2 * t + half + 1)
                    step(v.tensor_tensor(h_n[:, at], h_n[:, at], ln_gain[:].unsqueeze(1).to_broadcast([P, 2, D]), ALU.mult))
                    v.tensor_tensor(x_all[:, t, at].rearrange("p c d -> p (c d)"),
                                    x_all[:, t, at].rearrange("p c d -> p (c d)"),
                                    h_n[:, at].rearrange("p c d -> p (c d)"), ALU.add).then_inc(x1_ok, 1)

            low_x(0)
            group_combine(B - 1, 1)
            statsB(B - 2, 0)
            statsB(B - 2, 1)
            dve.wait_ge(stB_ok, 2 * (B - 1))
            meanB()
            norm_max(B - 1)
            norm_eps(B - 1)
            norm_divide(B - 1)
            statsA(B - 1)
            dve.wait_ge(stA_ok, B)
            meanA()
            step(v.tensor_copy(weight[:, :, 0], tanhs[:, 1:2].to_broadcast([P, B * C])))
            square(0, 0)
            square(0, 1)
            accumulate(0, 0)
            last_residual()
            dve.wait_ge(rsB_ok, B - 1)
            statsB(B - 1, 0)
            statsB(B - 1, 1)
            dve.wait_ge(stB_ok, 2 * B)
            meanB()
            accumulate(0, 1)
            square(0, 2)
            dve.wait_ge(before_ok, 1)
            weigh_experts(1, slice(0, 3 * C))
            square(0, 3)
            accumulate(0, 2)
            square(1, 0)
            accumulate(0, 3)
            square(1, 1)
            accumulate(1, 0)
            weigh_experts(2, slice(3 * C, B * C))
            square(1, 2)
            accumulate(1, 1)
            square(1, 3)
            accumulate(1, 2)
            with dve.Fori(2, NE) as e:
                square(e, 0)
                accumulate(e - 1, B - 1)
                for b in range(1, B):
                    square(e, b)
                    accumulate(e, b - 1)
            accumulate(NE - 1, B - 1)


def kernel(x, ctx_1024, g_xattn, g_ffn, L0_xattn_igate_w, L0_xattn_igate_b, L0_xattn_fgate_w, L0_xattn_fgate_b,
           L0_xattn_ln_scale, L0_ffn_gate_w, L0_ffn_lb_bias, L0_ffn_w1, L0_ffn_w2, L0_ffn_cfc, L0_ffn_cproj):
    import concourse.bacc as bacc
    from concourse.bass_utils import run_bass_kernel_spmd

    a = np.asarray

    def halves(w):
        return a(w).transpose(2, 0, 1).reshape(KC, P, -1, w.shape[1]).transpose(1, 2, 0, 3)

    up = np.concatenate([halves(a(L0_ffn_cfc)[None]), halves(a(L0_ffn_w1))], 1)
    down = np.concatenate([halves(a(L0_ffn_cproj)[None]), halves(a(L0_ffn_w2))], 1)
    gates = np.concatenate([a(L0_xattn_igate_w), a(L0_xattn_fgate_w)], 0)
    arrays = {
        "x": a(x),
        "ctx": a(ctx_1024),
        "ctxT": a(ctx_1024).transpose(0, 2, 1),
        "experts": np.stack([up, down], 2),
        "gate_w": gates.T.reshape(3 * KC, P, 2 * NH).transpose(1, 0, 2),
        "gate_b": np.stack([np.tile(a(L0_xattn_igate_b), B), np.tile(a(L0_xattn_fgate_b), B)], 1),
        "row": np.concatenate([a(L0_xattn_ln_scale), a(L0_ffn_lb_bias), a(g_xattn), a(g_ffn)])[None],
        "route_w": a(L0_ffn_gate_w).T.reshape(KC, P, E).transpose(1, 0, 2),
    }
    arrays = {n: np.ascontiguousarray(v) for n, v in arrays.items()}
    nc = bacc.Bacc("TRN2", target_bir_lowering=False, num_devices=1)
    args = {n: nc.dram_tensor(n, v.shape, F32, kind="ExternalInput").ap() for n, v in arrays.items()}
    out = nc.dram_tensor("out", (B, S, D), F32, kind="ExternalOutput").ap()
    gated_block(nc, out=out, **args)
    r = run_bass_kernel_spmd(nc, [arrays], core_ids=[0])
    return r.results[0]["out"]
```
